# Optimizing a Trainium2 kernel written in Bass

```python
import numpy as np
import jax
import jax.numpy as jnp

def _softmax(x, axis=-1):
    return jax.nn.softmax(x, axis=axis)

def _gelu(x):
    return jax.nn.gelu(x, approximate=True)

def _silu(x):
    return jax.nn.silu(x)

def _sigmoid(x):
    return jax.nn.sigmoid(x)

def _layernorm(x, axis=-1, eps=1e-05):
    m = jnp.mean(x, axis=axis, keepdims=True)
    v = jnp.var(x, axis=axis, keepdims=True)
    return (x - m) / jnp.sqrt(v + eps)

def _scatter_add(tgt, idx, src, axis=0):
    return tgt.at[idx].add(src)

def _segment_sum(src, seg, n):
    return jax.ops.segment_sum(src, seg, n)
kernel_name = 'mk_cond_seq_d2_seqx_r4_9ca845'

def setup_inputs(seed: int=0):
    np.random.seed(seed)
    _w = jnp.asarray

    def _rec_inputs():
        import jax
        import jax.numpy as jnp
        _rk = jax.random.key(seed)
        x = -0.0002928 + 1 * jax.random.normal(jax.random.fold_in(_rk, 1), (4, 512, 256), jnp.float32)
        _lenS = 512 - jax.random.randint(jax.random.fold_in(_rk, 7), (4,), 0, max(1, 512 // 4) + 1, jnp.int32)
        _lenS2 = 512 - jax.random.randint(jax.random.fold_in(_rk, 8), (4,), 0, max(1, 512 // 4) + 1, jnp.int32)
        itok_B_6_14 = jax.random.randint(jax.random.fold_in(_rk, 11), (4,), 6, 15, jnp.int32)
        condB_gatescore = jax.random.uniform(jax.random.fold_in(_rk, 12), (4,), jnp.float32, 0.0, 0.581427)
        return (x, itok_B_6_14, condB_gatescore)
    x, itok_B_6_14, condB_gatescore = _rec_inputs()

    def _L0_cond_setup():
        import jax, jax.numpy as jnp
        import numpy as np
        D = 256
        E = 8
        FF = 1024
        TOPK = 2
        S = 32
        SE = 64
        SH = 128
        B, T = (2, 512)

        def _forward(x, subject_ids, ln_g, ln_b, subj_emb, hyp_w1, hyp_b1, hyp_w2, hyp_b2, sty_w1, sty_b1, sty_w2, sty_b2, router_w, exp_w1, exp_b1, exp_w2, exp_b2):
            mu = x.mean(-1, keepdims=True)
            var = x.var(-1, keepdims=True)
            h = (x - mu) * jax.lax.rsqrt(var + 1e-05) * ln_g + ln_b
            m_t = h.mean(1, keepdims=True)
            v_t = h.var(1, keepdims=True)
            h_norm = (h - m_t) * jax.lax.rsqrt(v_t + 1e-08)
            se = subj_emb[subject_ids]
            hyp = jax.nn.relu(se @ hyp_w1 + hyp_b1) @ hyp_w2 + hyp_b2
            sty = jax.nn.relu(hyp @ sty_w1 + sty_b1) @ sty_w2 + sty_b2
            gamma, beta = jnp.split(sty, 2, axis=-1)
            gamma = jax.nn.softplus(gamma) + 1e-08
            h = h_norm * gamma[:, None, :] + beta[:, None, :]
            h_flat = h.reshape(-1, D)
            probs = jax.nn.softmax(h_flat @ router_w, axis=-1)
            gates, idx = jax.lax.top_k(probs, TOPK)
            gates = gates / gates.sum(-1, keepdims=True)
            N = h_flat.shape[0]
            combine = jnp.zeros((N, E), h_flat.dtype).at[jnp.arange(N)[:, None], idx].add(gates)
            hid = jax.nn.relu(jnp.einsum('nd,edf->nef', h_flat, exp_w1) + exp_b1)
            eout = jnp.einsum('nef,efd->ned', hid, exp_w2) + exp_b2
            y = jnp.einsum('ned,ne->nd', eout, combine)
            return x + y.reshape(x.shape)
        key = jax.random.key(seed)
        ks = jax.random.split(key, 16)
        n = lambda k, sh, s=0.02: jax.random.normal(k, sh, dtype=jnp.float32) * s
        return {'x': jax.random.normal(ks[0], (B, T, D), dtype=jnp.float32), 'subject_ids': jax.random.randint(ks[1], (B,), 0, S), 'ln_g': jnp.ones((D,), jnp.float32), 'ln_b': jnp.zeros((D,), jnp.float32), 'subj_emb': n(ks[2], (S, SE)), 'hyp_w1': n(ks[3], (SE, SH), 1.0 / np.sqrt(SE)), 'hyp_b1': jnp.zeros((SH,), jnp.float32), 'hyp_w2': n(ks[4], (SH, SH), 1.0 / np.sqrt(SH)), 'hyp_b2': jnp.zeros((SH,), jnp.float32), 'sty_w1': n(ks[5], (SH, SH // 2), 1.0 / np.sqrt(SH)), 'sty_b1': jnp.zeros((SH // 2,), jnp.float32), 'sty_w2': n(ks[6], (SH // 2, 2 * D), 1.0 / np.sqrt(SH // 2)), 'sty_b2': jnp.zeros((2 * D,), jnp.float32), 'router_w': n(ks[7], (D, E), 1.0 / np.sqrt(D)), 'exp_w1': n(ks[8], (E, D, FF), 1.0 / np.sqrt(D)), 'exp_b1': jnp.zeros((E, FF), jnp.float32), 'exp_w2': n(ks[9], (E, FF, D), 1.0 / np.sqrt(FF)), 'exp_b2': jnp.zeros((E, D), jnp.float32)}
    _L0_cond_all = _L0_cond_setup()
    _L0_cond_in = {k: v for k, v in _L0_cond_all.items() if k in ('ln_g', 'ln_b', 'subj_emb', 'hyp_w1', 'hyp_b1', 'hyp_w2', 'hyp_b2', 'sty_w1', 'sty_b1', 'sty_w2', 'sty_b2', 'router_w', 'exp_w1', 'exp_b1', 'exp_w2', 'exp_b2')}
    del _L0_cond_all

    def _L1_cond_setup():
        import jax, jax.numpy as jnp
        import numpy as np
        D_MODEL = 256
        N_HEADS = 16
        D_HEAD = D_MODEL // N_HEADS
        D_FF = 1024
        EPS = 1e-05

        def layernorm(x, gamma, beta):
            mu = jnp.mean(x, axis=-1, keepdims=True)
            var = jnp.var(x, axis=-1, keepdims=True)
            return (x - mu) * jax.lax.rsqrt(var + EPS) * gamma + beta
        key = jax.random.key(seed)
        ks = jax.random.split(key, 16)
        B, T = (4, 512)
        s = 1.0 / np.sqrt(D_MODEL)
        sf = 1.0 / np.sqrt(D_FF)
        return {'x': jax.random.normal(ks[0], (B, T, D_MODEL), jnp.float32), 'gate_score': jax.random.uniform(ks[1], (B,), jnp.float32), 'Wq': jax.random.normal(ks[2], (D_MODEL, D_MODEL), jnp.float32) * s, 'bq': jnp.zeros((D_MODEL,), jnp.float32), 'Wk': jax.random.normal(ks[3], (D_MODEL, D_MODEL), jnp.float32) * s, 'bk': jnp.zeros((D_MODEL,), jnp.float32), 'Wv': jax.random.normal(ks[4], (D_MODEL, D_MODEL), jnp.float32) * s, 'bv': jnp.zeros((D_MODEL,), jnp.float32), 'Wo': jax.random.normal(ks[5], (D_MODEL, D_MODEL), jnp.float32) * s, 'bo': jnp.zeros((D_MODEL,), jnp.float32), 'W1': jax.random.normal(ks[6], (D_MODEL, D_FF), jnp.float32) * s, 'b1': jnp.zeros((D_FF,), jnp.float32), 'W2': jax.random.normal(ks[7], (D_FF, D_MODEL), jnp.float32) * sf, 'b2': jnp.zeros((D_MODEL,), jnp.float32), 'gamma1': jnp.ones((D_MODEL,), jnp.float32), 'beta1': jnp.zeros((D_MODEL,), jnp.float32), 'gamma2': jnp.ones((D_MODEL,), jnp.float32), 'beta2': jnp.zeros((D_MODEL,), jnp.float32)}
    _L1_cond_all = _L1_cond_setup()
    _L1_cond_in = {k: v for k, v in _L1_cond_all.items() if k in ('Wq', 'bq', 'Wk', 'bk', 'Wv', 'bv', 'Wo', 'bo', 'W1', 'b1', 'W2', 'b2', 'gamma1', 'beta1', 'gamma2', 'beta2')}
    del _L1_cond_all
    return {'x': x, 'itok_B_6_14': itok_B_6_14, 'condB_gatescore': condB_gatescore, 'L0_cond_ln_g': _L0_cond_in['ln_g'], 'L0_cond_ln_b': _L0_cond_in['ln_b'], 'L0_cond_subj_emb': _L0_cond_in['subj_emb'], 'L0_cond_hyp_w1': _L0_cond_in['hyp_w1'], 'L0_cond_hyp_b1': _L0_cond_in['hyp_b1'], 'L0_cond_hyp_w2': _L0_cond_in['hyp_w2'], 'L0_cond_hyp_b2': _L0_cond_in['hyp_b2'], 'L0_cond_sty_w1': _L0_cond_in['sty_w1'], 'L0_cond_sty_b1': _L0_cond_in['sty_b1'], 'L0_cond_sty_w2': _L0_cond_in['sty_w2'], 'L0_cond_sty_b2': _L0_cond_in['sty_b2'], 'L0_cond_router_w': _L0_cond_in['router_w'], 'L0_cond_exp_w1': _L0_cond_in['exp_w1'], 'L0_cond_exp_b1': _L0_cond_in['exp_b1'], 'L0_cond_exp_w2': _L0_cond_in['exp_w2'], 'L0_cond_exp_b2': _L0_cond_in['exp_b2'], 'L1_cond_Wq': _L1_cond_in['Wq'], 'L1_cond_bq': _L1_cond_in['bq'], 'L1_cond_Wk': _L1_cond_in['Wk'], 'L1_cond_bk': _L1_cond_in['bk'], 'L1_cond_Wv': _L1_cond_in['Wv'], 'L1_cond_bv': _L1_cond_in['bv'], 'L1_cond_Wo': _L1_cond_in['Wo'], 'L1_cond_bo': _L1_cond_in['bo'], 'L1_cond_W1': _L1_cond_in['W1'], 'L1_cond_b1': _L1_cond_in['b1'], 'L1_cond_W2': _L1_cond_in['W2'], 'L1_cond_b2': _L1_cond_in['b2'], 'L1_cond_gamma1': _L1_cond_in['gamma1'], 'L1_cond_beta1': _L1_cond_in['beta1'], 'L1_cond_gamma2': _L1_cond_in['gamma2'], 'L1_cond_beta2': _L1_cond_in['beta2']}

def reference(x, itok_B_6_14, condB_gatescore, L0_cond_ln_g, L0_cond_ln_b, L0_cond_subj_emb, L0_cond_hyp_w1, L0_cond_hyp_b1, L0_cond_hyp_w2, L0_cond_hyp_b2, L0_cond_sty_w1, L0_cond_sty_b1, L0_cond_sty_w2, L0_cond_sty_b2, L0_cond_router_w, L0_cond_exp_w1, L0_cond_exp_b1, L0_cond_exp_w2, L0_cond_exp_b2, L1_cond_Wq, L1_cond_bq, L1_cond_Wk, L1_cond_bk, L1_cond_Wv, L1_cond_bv, L1_cond_Wo, L1_cond_bo, L1_cond_W1, L1_cond_b1, L1_cond_W2, L1_cond_b2, L1_cond_gamma1, L1_cond_beta1, L1_cond_gamma2, L1_cond_beta2):
    import jax
    import jax.numpy as jnp

    def _L0_cond_ref(x, subject_ids, ln_g, ln_b, subj_emb, hyp_w1, hyp_b1, hyp_w2, hyp_b2, sty_w1, sty_b1, sty_w2, sty_b2, router_w, exp_w1, exp_b1, exp_w2, exp_b2):
        import jax, jax.numpy as jnp
        import numpy as np
        D = 256
        E = 8
        FF = 1024
        TOPK = 2
        S = 32
        SE = 64
        SH = 128
        B, T = (2, 512)

        def _forward(x, subject_ids, ln_g, ln_b, subj_emb, hyp_w1, hyp_b1, hyp_w2, hyp_b2, sty_w1, sty_b1, sty_w2, sty_b2, router_w, exp_w1, exp_b1, exp_w2, exp_b2):
            mu = x.mean(-1, keepdims=True)
            var = x.var(-1, keepdims=True)
            h = (x - mu) * jax.lax.rsqrt(var + 1e-05) * ln_g + ln_b
            m_t = h.mean(1, keepdims=True)
            v_t = h.var(1, keepdims=True)
            h_norm = (h - m_t) * jax.lax.rsqrt(v_t + 1e-08)
            se = subj_emb[subject_ids]
            hyp = jax.nn.relu(se @ hyp_w1 + hyp_b1) @ hyp_w2 + hyp_b2
            sty = jax.nn.relu(hyp @ sty_w1 + sty_b1) @ sty_w2 + sty_b2
            gamma, beta = jnp.split(sty, 2, axis=-1)
            gamma = jax.nn.softplus(gamma) + 1e-08
            h = h_norm * gamma[:, None, :] + beta[:, None, :]
            h_flat = h.reshape(-1, D)
            probs = jax.nn.softmax(h_flat @ router_w, axis=-1)
            gates, idx = jax.lax.top_k(probs, TOPK)
            gates = gates / gates.sum(-1, keepdims=True)
            N = h_flat.shape[0]
            combine = jnp.zeros((N, E), h_flat.dtype).at[jnp.arange(N)[:, None], idx].add(gates)
            hid = jax.nn.relu(jnp.einsum('nd,edf->nef', h_flat, exp_w1) + exp_b1)
            eout = jnp.einsum('nef,efd->ned', hid, exp_w2) + exp_b2
            y = jnp.einsum('ned,ne->nd', eout, combine)
            return x + y.reshape(x.shape)
        return _forward(x, subject_ids, ln_g, ln_b, subj_emb, hyp_w1, hyp_b1, hyp_w2, hyp_b2, sty_w1, sty_b1, sty_w2, sty_b2, router_w, exp_w1, exp_b1, exp_w2, exp_b2)

    def _L1_cond_ref(x, gate_score, Wq, bq, Wk, bk, Wv, bv, Wo, bo, W1, b1, W2, b2, gamma1, beta1, gamma2, beta2):
        import jax, jax.numpy as jnp
        import numpy as np
        D_MODEL = 256
        N_HEADS = 16
        D_HEAD = D_MODEL // N_HEADS
        D_FF = 1024
        EPS = 1e-05

        def layernorm(x, gamma, beta):
            mu = jnp.mean(x, axis=-1, keepdims=True)
            var = jnp.var(x, axis=-1, keepdims=True)
            return (x - mu) * jax.lax.rsqrt(var + EPS) * gamma + beta
        B, T, C = x.shape
        h = layernorm(x, gamma1, beta1)
        Q = (h @ Wq + bq).reshape(B, T, N_HEADS, D_HEAD).transpose(0, 2, 1, 3)
        K = (h @ Wk + bk).reshape(B, T, N_HEADS, D_HEAD).transpose(0, 2, 1, 3)
        V = (h @ Wv + bv).reshape(B, T, N_HEADS, D_HEAD).transpose(0, 2, 1, 3)
        scores = jnp.einsum('bhqd,bhkd->bhqk', Q, K) / np.sqrt(D_HEAD)
        causal = jnp.tril(jnp.ones((T, T), dtype=bool))
        scores = jnp.where(causal, scores, -jnp.inf)
        attn = jax.nn.softmax(scores, axis=-1)
        ctx = jnp.einsum('bhqk,bhkd->bhqd', attn, V)
        ctx = ctx.transpose(0, 2, 1, 3).reshape(B, T, C)
        attn_out = ctx @ Wo + bo
        x1 = x + attn_out
        h2 = layernorm(x1, gamma2, beta2)
        ff = jax.nn.gelu(h2 @ W1 + b1, approximate=False) @ W2 + b2
        x2 = x1 + ff
        g = gate_score[:, None, None]
        return x + g * (x2 - x)
    x = _L0_cond_ref(x, itok_B_6_14, L0_cond_ln_g, L0_cond_ln_b, L0_cond_subj_emb, L0_cond_hyp_w1, L0_cond_hyp_b1, L0_cond_hyp_w2, L0_cond_hyp_b2, L0_cond_sty_w1, L0_cond_sty_b1, L0_cond_sty_w2, L0_cond_sty_b2, L0_cond_router_w, L0_cond_exp_w1, L0_cond_exp_b1, L0_cond_exp_w2, L0_cond_exp_b2)
    x = _L1_cond_ref(x, condB_gatescore, L1_cond_Wq, L1_cond_bq, L1_cond_Wk, L1_cond_bk, L1_cond_Wv, L1_cond_bv, L1_cond_Wo, L1_cond_bo, L1_cond_W1, L1_cond_b1, L1_cond_W2, L1_cond_b2, L1_cond_gamma1, L1_cond_beta1, L1_cond_gamma2, L1_cond_beta2)
    return x

_drawn_inputs = setup_inputs


def setup_inputs(seed=0):
    import zlib

    import numpy as np

    out = dict(_drawn_inputs(seed))
    spreads = {'L0_cond_ln_g': (1.0, 0.6),
     'L0_cond_ln_b': (0.0, 0.8),
     'L0_cond_hyp_b1': (0.0, 0.1),
     'L0_cond_hyp_b2': (0.0, 0.1),
     'L0_cond_sty_b1': (0.0, 0.1),
     'L0_cond_sty_b2': (0.0, 0.1),
     'L0_cond_exp_b1': (0.0, 0.1),
     'L0_cond_exp_b2': (0.0, 0.1),
     'L1_cond_bq': (0.0, 0.8),
     'L1_cond_bk': (0.0, 0.8),
     'L1_cond_bv': (0.0, 0.1),
     'L1_cond_bo': (0.0, 0.1),
     'L1_cond_b1': (0.0, 0.388),
     'L1_cond_b2': (0.0, 0.269),
     'L1_cond_gamma1': (1.0, 0.6),
     'L1_cond_beta1': (0.0, 0.1),
     'L1_cond_gamma2': (1.0, 0.2),
     'L1_cond_beta2': (0.0, 0.364)}
    factors = {}
    for name, (base, spread) in spreads.items():
        noise = np.random.default_rng([zlib.crc32(name.encode()), seed]).standard_normal(out[name].shape)
        drawn = base * np.exp(spread * noise) if base else spread * noise
        out[name] = jnp.asarray(drawn.astype(out[name].dtype))
    for name, factor in factors.items():
        out[name] = (out[name] * factor).astype(out[name].dtype)
    return out
```

```python
import concourse.bass as bass
from concourse import mybir
from contextlib import ExitStack

F32, F16, BF16, I32 = mybir.dt.float32, mybir.dt.float16, mybir.dt.bfloat16, mybir.dt.int32
U32 = mybir.dt.uint32
ALU = mybir.AluOpType
ACT = mybir.ActivationFunctionType
AX = mybir.AxisListType

P = 128
B, T, D = 4, 512, 256
N = B * T
NT = N // P
TPB = T // P
KD = D // P
E, FF = 8, 1024
FC = FF // P
S, SE, SH = 32, 64, 128
BLK = 256
TOPK = 2
MAXBLK = (N * TOPK + (BLK - 1) * E) // BLK
MINBLK = N * TOPK // BLK
XBLK = MAXBLK + 2
WROWS = ("Wq", "Wk", "Wv", "Wo")
BROWS = ("bq", "bk", "bv", "bo", "b2")
H, HD = 16, D // 16
HG = 4
G = H // HG
Q32 = 32
NEG = -1e30
CREDIT = 1
WS = 32.0
MS = WS * WS


class Shared:
    pass


def linked(eng, sem):
    count = [0]

    def link(ins):
        count[0] += 1
        ins.then_inc(sem, 1)
        eng.wait_ge(sem, count[0])
    return link


def layer1_weights(nc, a, m, c, wf, bf, f1, f2):
    def sb(name, shape, dt=F32):
        return c.enter_context(nc.sbuf_tensor(name, shape, dt))

    def sem(name):
        return c.enter_context(nc.semaphore(name))

    rows_of = lambda t: t[0:2, :, :].rearrange("p k f -> p (k f)")[:, 0:len(BROWS) * D].rearrange("p (n d) -> p n d", d=D)
    bh, bl = rows_of(m.w1h[1]), rows_of(m.w1l[1])
    w_in, f_in, b_in = sem("l1_w_in"), sem("l1_f_in"), sem("l1_b_in")
    hi_made, chain, zero_made, done = sem("l1_hi"), sem("l1_chain"), sem("l1_zero"), sem("l1_masks")

    def loads(sp):
        for n, w in enumerate(WROWS):
            sp.dma_start(wf[:, n, :, :], a["L1_cond_" + w].rearrange("(k p) d -> p k d", p=P)).then_inc(w_in, 16)
        for n, w in enumerate(BROWS):
            sp.dma_start(bf[:, n, :], a["L1_cond_" + w].rearrange("(o d) -> o d", o=1).broadcast_to([2, D])).then_inc(b_in, 16)
        sp.dma_start(m.g1[:, :], a["L1_cond_gamma1"].rearrange("(k p) -> p k", p=P), allow_slow_non_contiguous=True).then_inc(b_in, 16)
        sp.dma_start(m.be1[:, :], a["L1_cond_beta1"].rearrange("(k p) -> p k", p=P), allow_slow_non_contiguous=True).then_inc(b_in, 16)
        sp.dma_start(m.g2[:, :], a["L1_cond_gamma2"].rearrange("(k p) -> p k", p=P), allow_slow_non_contiguous=True).then_inc(b_in, 16)
        sp.dma_start(m.be2[:, :], a["L1_cond_beta2"].rearrange("(k p) -> p k", p=P), allow_slow_non_contiguous=True).then_inc(b_in, 16)
        sp.dma_start(m.bff[:, :], a["L1_cond_b1"].rearrange("(k p) -> p k", p=P), allow_slow_non_contiguous=True).then_inc(b_in, 16)
        sp.dma_start(m.gs[:, :], a["condB_gatescore"].rearrange("(o b) -> o b", o=1).broadcast_to([P, B])).then_inc(b_in, 16)
        sp.dma_start(f1[:, :, :], a["L1_cond_W1"].rearrange("(k p) f -> p k f", p=P)).then_inc(f_in, 16)
        sp.dma_start(f2[:, :, :], a["L1_cond_W2"].rearrange("(k p) d -> p k d", p=P)).then_inc(f_in, 16)

    def twice(ap, r):
        return ap.rearrange("p k (h r d) -> p k h r d", r=2, d=HD)[:, :, :, r, :]

    def heads(ap):
        return ap.rearrange("p k (h d) -> p k h d", d=HD)

    def constants(pool):
        link = linked(pool, done)
        nc.gpsimd.memset(m.brow[:, :, :], 0.0).then_inc(zero_made, 1)
        link(nc.gpsimd.memset(m.vp[:, :, :, HD:Q32], 0.0))
        link(nc.gpsimd.memset(m.vp[:, :, :, HD:HD + 1], 1.0))
        link(nc.gpsimd.memset(m.nmp[:, :, :], 0.0))
        for t, rest, first in ((m.msign, -1.0, 1.0), (m.mlow, 1.0, 0.0), (m.mfirst, 0.0, 1.0)):
            link(nc.gpsimd.memset(t[:, :], rest))
            for q in range(0, P, Q32):
                link(nc.gpsimd.memset(t[q:q + HD, :], first))
        link(nc.gpsimd.memset(m.kconst[:, :], 0.0))
        for q in range(0, P, Q32):
            link(nc.gpsimd.memset(m.kconst[q:q + HD + 2, :], MS))
            link(nc.gpsimd.memset(m.kconst[q:q + HD, :], 0.0))
        link(nc.gpsimd.tensor_copy(m.identb[:, :], m.ident[:, :]))
        link(nc.gpsimd.memset(m.future[:, :], 0.0))
        link(nc.gpsimd.affine_select(out=m.future[:, :], in_=m.future[:, :], compare_op=ALU.is_ge, fill=NEG,
                                     base=0, pattern=[[-1, P]], channel_multiplier=1))

    def highs(act):
        act.wait_ge(w_in, 16 * len(WROWS))
        for n, (hi, _) in enumerate((m.wq, m.wk)):
            for r in range(2):
                nc.scalar.activation(twice(hi[:, :, :], r), heads(wf[:, n, :, :]), ACT.Copy, scale=WS).then_inc(hi_made, 1)
        for n, (hi, _) in enumerate((m.wv, m.wo)):
            nc.scalar.activation(hi[:, :, :], wf[:, 2 + n, :, :], ACT.Copy, scale=WS).then_inc(hi_made, 1)
        act.wait_ge(f_in, 32)
        nc.scalar.activation(m.f1h[:, :, :], f1[:, :, :], ACT.Copy, scale=WS).then_inc(hi_made, 1)
        nc.scalar.activation(m.f2h[:, :, :], f2[:, :, :], ACT.Copy, scale=WS).then_inc(hi_made, 1)

    def lows(dve):
        v = nc.vector
        link = linked(dve, chain)
        dve.wait_ge(w_in, 16 * len(WROWS))

        def low(out, full, hi):
            return v.scalar_tensor_tensor(out=out, in0=full, scalar=WS, in1=hi, op0=ALU.mult, op1=ALU.subtract)
        for n, (hi, lo) in enumerate((m.wq, m.wk)):
            for r in range(2):
                dve.wait_ge(hi_made, 2 * n + r + 1)
                for k in range(KD):
                    low(twice(lo[:, k:k + 1, :], r).squeeze(1), heads(wf[:, n, k:k + 1, :]).squeeze(1),
                        twice(hi[:, k:k + 1, :], r).squeeze(1))
        for n, (hi, lo) in enumerate((m.wv, m.wo)):
            dve.wait_ge(hi_made, 5 + n)
            low(lo[:, :, :], wf[:, 2 + n, :, :], hi[:, :, :])
        dve.wait_ge(hi_made, 7)
        low(m.f1l[:, :, :], f1[:, :, :], m.f1h[:, :, :])
        dve.wait_ge(hi_made, 8)
        low(m.f2l[:, :, :], f2[:, :, :], m.f2h[:, :, :])
        dve.wait_ge(b_in, 16 * (len(BROWS) + 6))
        dve.wait_ge(zero_made, 1)
        link(v.tensor_scalar(bh[:, :, :], bf[:, :, :], WS, None, ALU.mult))
        link(low(bl[:, :, :], bf[:, :, :], bh[:, :, :]))
        link(v.tensor_scalar(bl[:, :, :], bl[:, :, :], m.ident[0:2, 1:2], None, ALU.mult))
        link(v.scalar_tensor_tensor(out=m.brow[0:2, :, :], in0=bh[:, :, :], scalar=m.ident[0:2, 0:1], in1=bl[:, :, :],
                                    op0=ALU.mult, op1=ALU.add))
        for r in range(2):
            link(v.tensor_copy(twice(m.bdup[:, :, :], r), heads(m.brow[:, 0:2, :])))
    return loads, constants, highs, lows


def front(nc, a, m):
    with ExitStack() as c:
        def sb(name, shape, dt=F32):
            return c.enter_context(nc.sbuf_tensor(name, shape, dt))

        def ps(name, shape, dt=F32):
            return c.enter_context(nc.psum_tensor(name, shape, dt))

        def sem(name):
            return c.enter_context(nc.semaphore(name))

        x, z = m.x, sb("z", [P, NT, D])
        hT = sb("hT", [P, KD, N])
        stats = sb("stats", [P, NT, 6])
        mv = sb("mv", [P, NT, 2])
        rstd = sb("rstd", [P, NT])
        tstats = sb("tstats", [P, KD * B, 6])
        tmv = sb("tmv", [P, KD * B, 2])
        scaleA, biasB = sb("scaleA", [P, KD * B]), sb("biasB", [P, KD * B])
        lng, lnb = sb("lng", [P, KD]), sb("lnb", [P, KD])
        rw = sb("rw", [P, KD, E])
        emb = sb("emb", [S, SE])
        hw1, hb1 = sb("hw1", [SE, SH]), sb("hb1", [SH, 1])
        hw2, hb2 = sb("hw2", [SH, SH]), sb("hb2", [SH, 1])
        sw1, sb1 = sb("sw1", [SH, SH // 2]), sb("sb1", [SH // 2, 1])
        sw2, sb2 = sb("sw2", [SH // 2, 2 * D]), sb("sb2", [P, 2 * KD])
        ids, idsf = sb("ids", [S, B], I32), sb("idsf", [S, B])
        subj, onehot = sb("subj", [S, 1]), sb("onehot", [S, B])
        st_a, st_b = sb("st_a", [P, B]), sb("st_b", [P, B])
        st_c, st_d = sb("st_c", [P, B]), sb("st_d", [P, B])
        sty = sb("sty", [P, 2 * KD, B])
        spa, spb = sb("spa", [P, KD, B]), sb("spb", [P, KD, B])
        gam = sb("gam", [P, KD, B])
        rows = sb("rows", [P, NT, 2 * D], F16)
        b1s, b1h, b1l = sb("b1s", [P, E * FF // P]), sb("b1h", [P, E * FF // P], F16), sb("b1l", [P, E * FF // P], F16)
        b2s, b2h, b2l = sb("b2s", [P, E * D // P]), sb("b2h", [P, E * D // P], F16), sb("b2l", [P, E * D // P], F16)
        zeros = m.w2h[1][:, :, :].rearrange("p (g q) d -> p g (q d)", q=2)
        upper, ones16 = sb("upper", [P, P], BF16), sb("onesb", [P, P], BF16)
        seven = sb("seven", [P, NT, E])
        blkno = sb("blkno", [P, E])
        prob, rt0, rt1 = sb("prob", [P, NT, E]), sb("rt0", [P, NT, E]), sb("rt1", [P, NT, E])
        M1, M2 = sb("M1", [P, NT, E]), sb("M2", [P, NT, E])
        Mb = sb("Mb", [P, NT, E], BF16)
        tot = [sb(f"tot{i}", [P, NT, E]) for i in range(5)]
        red, p1, p2 = sb("red", [P, NT]), sb("p1", [P, NT]), sb("p2", [P, NT])
        cnt, cnti, cntj, nbf = sb("cnt", [P, E]), sb("cnti", [P, E], I32), sb("cntj", [P, E], I32), sb("nbf", [P, E])
        cum = [sb(f"cum{i}", [P, E]) for i in range(4)]
        base = sb("base", [P, E])
        slotf = sb("slotf", [P, NT])
        pt = [ps(f"pt{i}", [P, 512]) for i in range(4)]
        psty, plog, prank, ptot = ps("psty", [P, 512]), ps("plog", [P, 512]), ps("prank", [P, 512]), ps("ptot", [P, 512])

        x_in = [sem(f"x_in{i}") for i in range(4)]
        small_in, bias_in = sem("small_in"), sem("bias_in")
        consts, seven_made, zeros_made = sem("consts"), sem("seven_made"), sem("zeros_made")
        z_made, zT_made, hT_made = sem("z_made"), sem("zT_made"), sem("hT_made")
        hmod_made, hback_made, hi_made, rows_made = sem("hmod_made"), sem("hback_made"), sem("hi_made"), sem("rows_made")
        sty_ps, sty_sb, sp_step, sp_done = sem("sty_ps"), sem("sty_sb"), sem("sp_step"), sem("sp_done")
        logits, exps_in, exps, onehots, ranks = sem("logits"), sem("exps_in"), sem("exps"), sem("onehots"), sem("ranks")
        slots_made, scattered, zeroed = sem("slots_made"), sem("scattered"), sem("zeroed")
        dch, bsplit_hi, bsplit, brow_in, brow_zero = sem("dch"), sem("bsplit_hi"), sem("bsplit"), sem("brow_in"), sem("brow_zero")
        first_hi = sem("first_hi")
        pch, yzeroed = sem("pch"), sem("yzeroed")
        loads1, constants1, highs1, lows1 = layer1_weights(
            nc, a, m, c, z[:, 0:len(WROWS) * KD, :].rearrange("p (n k) d -> p n k d", k=KD),
            z[0:2, len(WROWS) * KD:len(WROWS) * KD + len(BROWS), :], m.w1f[1], m.w2f[1])
        var_made, rstd_made, tvar_made, trstd_made = sem("var_made"), sem("rstd_made"), sem("tvar_made"), sem("trstd_made")

        block = c.enter_context(nc.Block())
        xt = a["x"].rearrange("b (t p) d -> p (b t) d", p=P)
        col = lambda ap: ap.rearrange("(k p) -> p k", p=P)
        smalls = [
            (lng[:, :], col(a["L0_cond_ln_g"])), (lnb[:, :], col(a["L0_cond_ln_b"])),
            (emb[:, :], a["L0_cond_subj_emb"]),
            (hw1[:, :], a["L0_cond_hyp_w1"]), (hb1[:, :], a["L0_cond_hyp_b1"].rearrange("(p o) -> p o", o=1)),
            (hw2[:, :], a["L0_cond_hyp_w2"]), (hb2[:, :], a["L0_cond_hyp_b2"].rearrange("(p o) -> p o", o=1)),
            (sw1[:, :], a["L0_cond_sty_w1"]), (sb1[:, :], a["L0_cond_sty_b1"].rearrange("(p o) -> p o", o=1)),
            (sw2[:, :], a["L0_cond_sty_w2"]), (sb2[:, :], col(a["L0_cond_sty_b2"])),
            (rw[:, :, :], a["L0_cond_router_w"].rearrange("(k p) e -> p k e", p=P)),
            (ids[:, :], a["itok_B_6_14"].rearrange("(o b) -> o b", o=1).broadcast_to([S, B])),
        ]
        SMALL = 16 * len(smalls)

        @block.sync
        def _(sp):
            for b in range(B):
                sp.dma_start(x[:, b * TPB:(b + 1) * TPB, :], xt[:, b * TPB:(b + 1) * TPB, :]).then_inc(x_in[b], 16)
            for dst, src in smalls:
                sp.dma_start(dst, src, allow_slow_non_contiguous=True).then_inc(small_in, 16)
            sp.dma_start(b1s[:, :], a["L0_cond_exp_b1"].rearrange("e (q f) -> (e q) f", q=P // E)).then_inc(bias_in, 16)
            sp.dma_start(b2s[:, :], a["L0_cond_exp_b2"].rearrange("e (q f) -> (e q) f", q=P // E)).then_inc(bias_in, 16)
            sp.dma_start(m.w1f[0][:, :, :], a["L0_cond_exp_w1"][0, :, :].rearrange("(k p) f -> p k f", p=P)).then_inc(m.first_w[0], 16)
            sp.dma_start(m.w2f[0][:, :, :], a["L0_cond_exp_w2"][0, :, :].rearrange("(k p) d -> p k d", p=P)).then_inc(m.first_w[1], 16)
            sp.wait_ge(zeros_made, 1)
            per = 4 * P
            for i in range(0, XBLK * BLK, per):
                n = min(per, XBLK * BLK - i)
                sp.dma_start(m.xs[i:i + n, :].rearrange("(g p) d -> p g d", p=P), zeros[:, 0:n // P, :]).then_inc(zeroed, 16)
            sp.dma_start(m.ys[MINBLK * BLK:MAXBLK * BLK, :].rearrange("(g p) d -> p g d", p=P),
                         zeros[:, 0:1, :].bitcast(F32).broadcast_to([P, (MAXBLK - MINBLK) * BLK // P, D])).then_inc(yzeroed, 16)
            sp.wait_ge(bsplit, 2)
            sp.wait_ge(brow_zero, 1)
            for r, (q1, q2) in enumerate(((b1h, b2h), (b1l, b2l))):
                sp.dma_start(m.b1row[r:r + 1, :], q1[:, :]).then_inc(brow_in, 16)
                sp.dma_start(m.b2row[r:r + 1, :], q2[:, :]).then_inc(brow_in, 16)
            sp.wait_ge(zT_made, KD * B)
            loads1(sp)
            sp.wait_ge(brow_in, 64)
            sp.wait_ge(yzeroed, 16)

        ZEROED = 16 * -(-XBLK * BLK // (4 * P))

        @block.gpsimd
        def _(pool):
            link = linked(pool, pch)
            link(nc.gpsimd.memset(m.ident[:, :], 0.0))
            link(nc.gpsimd.affine_select(out=m.ident[:, :], in_=m.ident[:, :], compare_op=ALU.not_equal, fill=1.0,
                                         base=0, pattern=[[-1, P]], channel_multiplier=1))
            link(nc.gpsimd.tensor_copy(m.ident16[:, :], m.ident[:, :]))
            link(nc.gpsimd.iota(subj[:, :], pattern=[[0, 1]], base=0, channel_multiplier=1, allow_small_or_imprecise_dtypes=True))
            link(nc.gpsimd.memset(m.ones16[:, :], 1.0))
            link(nc.gpsimd.memset(m.mhalf[:, :], -0.5))
            nc.gpsimd.memset(ones16[:, :], 1.0).then_inc(consts, 1)
            nc.gpsimd.memset(zeros[:, :, :], 0.0).then_inc(zeros_made, 1)
            for b in range(B):
                pool.wait_ge(var_made, b + 1)
                r = rstd[:, b * TPB:(b + 1) * TPB]
                link(nc.gpsimd.tensor_scalar(r, mv[:, b * TPB:(b + 1) * TPB, 1], 1e-5, None, ALU.add))
                nc.gpsimd.tensor_tensor(r, r, m.mhalf[:, 0:TPB], ALU.pow).then_inc(rstd_made, 1)
            link(nc.gpsimd.memset(upper[:, :], 1.0))
            nc.gpsimd.affine_select(out=upper[:, :], in_=upper[:, :], compare_op=ALU.is_gt, fill=0.0,
                                    base=0, pattern=[[1, P]], channel_multiplier=-1).then_inc(consts, 1)
            nc.gpsimd.iota(seven[:, :, :], pattern=[[0, NT], [-1, E]], base=E, channel_multiplier=0,
                           allow_small_or_imprecise_dtypes=True).then_inc(seven_made, 1)
            nc.gpsimd.memset(m.b2row[:, :], 0.0)
            nc.gpsimd.memset(m.b1row[:, :], 0.0).then_inc(brow_zero, 1)
            pool.wait_ge(tvar_made, 1)
            link(nc.gpsimd.tensor_scalar(scaleA[:, :], tmv[:, :, 1], 1e-8, None, ALU.add))
            nc.gpsimd.tensor_tensor(scaleA[:, :], scaleA[:, :], m.mhalf[:, :], ALU.pow).then_inc(trstd_made, 1)
            constants1(pool)
            pool.wait_ge(zeroed, ZEROED)
            pool.wait_ge(slots_made, 2)
            for t in range(NT):
                pool.wait_ge(rows_made, t // 2 + 1)
                for s in (m.slot1, m.slot2):
                    nc.gpsimd.indirect_dma_start(
                        out=m.xs[:, :], out_offset=bass.IndirectOffsetOnAxis(ap=s[:, t:t + 1], axis=0),
                        in_=rows[:, t, :], in_offset=None).then_inc(scattered, 16)
            pool.wait_ge(scattered, 16 * 2 * NT)

        @block.scalar
        def _(act):
            act.wait_ge(small_in, SMALL)
            for n in range(KD * B):
                act.wait_ge(zT_made, n + 1)
                k, b = n % KD, n // KD
                nc.scalar.activation(hT[:, k, b * T:(b + 1) * T], pt[n % 2][:, :], ACT.Identity,
                                     bias=lnb[:, k:k + 1], scale=lng[:, k:k + 1]).then_inc(hT_made, 1)
            act.wait_ge(sp_step, 1)
            nc.scalar.activation(spb[:, :, :], spa[:, :, :], ACT.Exp, scale=-1.0).then_inc(sp_done, 1)
            act.wait_ge(sp_done, 1)
            nc.scalar.activation(spa[:, :, :], spb[:, :, :], ACT.Ln, bias=1.0).then_inc(sp_done, 1)
            act.wait_ge(exps_in, 1)
            nc.scalar.activation(rt1[:, :, :], rt0[:, :, :], ACT.Exp).then_inc(exps, 1)
            for n in range(NT // 2):
                act.wait_ge(hback_made, n + 1)
                nc.scalar.activation(rows[:, 2 * n:2 * n + 2, 0:D], pt[2 + n % 2][:, :].rearrange("p (t d) -> p t d", t=2),
                                     ACT.Copy).then_inc(hi_made, 1)
            act.wait_ge(m.first_w[0], 16)
            nc.scalar.activation(m.w1h[0][:, :, :], m.w1f[0][:, :, :], ACT.Copy, scale=WS).then_inc(first_hi, 1)
            act.wait_ge(m.first_w[1], 16)
            nc.scalar.activation(m.w2h[0][:, :, :], m.w2f[0][:, :, :], ACT.Copy, scale=WS).then_inc(first_hi, 1)
            highs1(act)

        def bias_rows(dve, v, link):
            dve.wait_ge(bias_in, 32)
            for src, hi, lo, k in ((b1s, b1h, b1l, WS), (b2s, b2h, b2l, WS * WS)):
                link(v.tensor_scalar(hi[:, :], src[:, :], k, None, ALU.mult))
                v.scalar_tensor_tensor(out=lo[:, :], in0=src[:, :], scalar=k, in1=hi[:, :], op0=ALU.mult, op1=ALU.subtract).then_inc(bsplit, 1)

        @block.vector
        def _(dve):
            v = nc.vector
            link = linked(dve, dch)
            def statistics(b):
                dve.wait_ge(x_in[b], 16)
                for t in range(b * TPB, (b + 1) * TPB):
                    last = v.bn_stats(out=stats[:, t, :], in_=x[:, t, :])
                link(last)
                for t in range(b * TPB, (b + 1) * TPB):
                    last = v.bn_aggr(out=mv[:, t, :], in_=stats[:, t, :])
                last.then_inc(var_made, 1)
            statistics(0)
            for b in range(B):
                if b + 1 < B:
                    statistics(b + 1)
                dve.wait_ge(rstd_made, b + 1)
                for t in range(b * TPB, (b + 1) * TPB):
                    v.tensor_scalar(z[:, t, :], x[:, t, :], mv[:, t, 0:1], rstd[:, t:t + 1],
                                    ALU.subtract, ALU.mult).then_inc(z_made, 1)
            dve.wait_ge(small_in, SMALL)
            dve.wait_ge(consts, 1)
            link(v.tensor_copy(idsf[:, :], ids[:, :]))
            v.tensor_scalar(onehot[:, :], idsf[:, :], subj[:, 0:1], None, ALU.is_equal).then_inc(sty_sb, 1)
            dve.wait_ge(sty_ps, 1)
            v.tensor_copy(st_a[0:SE, :], psty[0:SE, 0:B]).then_inc(sty_sb, 1)
            dve.wait_ge(sty_ps, 2)
            v.tensor_scalar(st_b[:, :], psty[:, B:2 * B], hb1[:, 0:1], 0.0, ALU.add, ALU.max).then_inc(sty_sb, 1)
            dve.wait_ge(sty_ps, 3)
            v.tensor_scalar(st_c[:, :], psty[:, 2 * B:3 * B], hb2[:, 0:1], None, ALU.add).then_inc(sty_sb, 1)
            dve.wait_ge(sty_ps, 4)
            v.tensor_scalar(st_d[0:SH // 2, :], psty[0:SH // 2, 3 * B:4 * B], sb1[:, 0:1], 0.0, ALU.add, ALU.max).then_inc(sty_sb, 1)
            dve.wait_ge(sty_ps, 5)
            link(v.tensor_tensor(sty[:, :, :], psty[:, 16:16 + 2 * KD * B].rearrange("p (c b) -> p c b", b=B),
                                 sb2[:, :].unsqueeze(2).broadcast_to([P, 2 * KD, B]), ALU.add))
            v.scalar_tensor_tensor(out=spa[:, :, :], in0=sty[:, 0:KD, :], scalar=-1.0, in1=sty[:, 0:KD, :], op0=ALU.mult, op1=ALU.max).then_inc(sp_step, 1)
            for n in range(KD * B):
                dve.wait_ge(hT_made, n + 1)
                k, b = n % KD, n // KD
                last = v.bn_stats(out=tstats[:, n, :], in_=hT[:, k, b * T:(b + 1) * T])
            link(last)
            for n in range(KD * B):
                last = v.bn_aggr(out=tmv[:, n, :], in_=tstats[:, n, :])
            last.then_inc(tvar_made, 1)
            dve.wait_ge(sp_done, 2)
            link(v.scalar_tensor_tensor(out=gam[:, :, :], in0=sty[:, 0:KD, :], scalar=0.0, in1=spa[:, :, :], op0=ALU.max, op1=ALU.add))
            link(v.tensor_scalar(gam[:, :, :], gam[:, :, :], 1e-8, None, ALU.add))
            dve.wait_ge(trstd_made, 1)
            link(v.tensor_tensor(scaleA[:, :].rearrange("p (b k) -> p k b", k=KD), scaleA[:, :].rearrange("p (b k) -> p k b", k=KD),
                                 gam[:, :, :], ALU.mult))
            link(v.tensor_tensor(biasB[:, :], tmv[:, :, 0], scaleA[:, :], ALU.mult))
            link(v.tensor_tensor(biasB[:, :].rearrange("p (b k) -> p k b", k=KD), sty[:, KD:2 * KD, :],
                                 biasB[:, :].rearrange("p (b k) -> p k b", k=KD), ALU.subtract))
            for n in range(KD * B):
                k, b = n % KD, n // KD
                hs = hT[:, k, b * T:(b + 1) * T]
                v.tensor_scalar(hs, hs, scaleA[:, n:n + 1], biasB[:, n:n + 1], ALU.mult, ALU.add).then_inc(hmod_made, 1)
            bias_rows(dve, v, link)
            dve.wait_ge(logits, 1)
            lg = plog[:, 0:NT * E].rearrange("p (t e) -> p t e", e=E)
            bc = lambda ap: ap.unsqueeze(2).broadcast_to([P, NT, E])
            link(v.tensor_reduce(red[:, :], lg, axis=AX.X, op=ALU.max))
            v.tensor_tensor(rt0[:, :, :], lg, bc(red[:, :]), ALU.subtract).then_inc(exps_in, 1)
            dve.wait_ge(exps, 1)
            link(v.tensor_reduce(red[:, :], rt1[:, :, :], axis=AX.X, op=ALU.add))
            link(v.reciprocal(red[:, :], red[:, :]))
            link(v.tensor_tensor(prob[:, :, :], rt1[:, :, :], bc(red[:, :]), ALU.mult))
            dve.wait_ge(seven_made, 1)

            def first_of_max(p, value, onehot_):
                link(v.tensor_reduce(value[:, :], p[:, :, :], axis=AX.X, op=ALU.max))
                link(v.tensor_tensor(onehot_[:, :, :], p[:, :, :], bc(value[:, :]), ALU.is_equal))
                link(v.tensor_tensor(onehot_[:, :, :], onehot_[:, :, :], seven[:, :, :], ALU.mult))
                link(v.tensor_reduce(red[:, :], onehot_[:, :, :], axis=AX.X, op=ALU.max))
                link(v.tensor_tensor(onehot_[:, :, :], onehot_[:, :, :], bc(red[:, :]), ALU.is_equal))
            first_of_max(prob, p1, M1)
            link(v.scalar_tensor_tensor(out=rt0[:, :, :], in0=M1[:, :, :], scalar=-4.0, in1=prob[:, :, :], op0=ALU.mult, op1=ALU.add))
            first_of_max(rt0, p2, M2)
            v.tensor_tensor(Mb[:, :, :], M1[:, :, :], M2[:, :, :], ALU.add).then_inc(onehots, 1)
            link(v.tensor_tensor(red[:, :], p1[:, :], p2[:, :], ALU.add))
            link(v.reciprocal(red[:, :], red[:, :]))
            for g, p in ((m.gate1, p1), (m.gate2, p2)):
                link(v.scalar_tensor_tensor(out=g[:, :], in0=p[:, :], scalar=1.0 / (WS * WS), in1=red[:, :], op0=ALU.mult, op1=ALU.mult))
            dve.wait_ge(ranks, 2)
            link(v.tensor_copy(tot[0][:, :, :], ptot[:, 0:NT * E].rearrange("p (t e) -> p t e", e=E)))
            for i, s in enumerate((1, 2, 4, 8)):
                v.tensor_copy(tot[i + 1][:, 0:s, :], tot[i][:, 0:s, :])
                link(v.tensor_tensor(tot[i + 1][:, s:, :], tot[i][:, s:, :], tot[i][:, :NT - s, :], ALU.add))
            link(v.tensor_scalar(cnti[:, :], tot[4][:, NT - 1, :], float(BLK - 1), None, ALU.add))
            link(v.tensor_scalar(cntj[:, :], cnti[:, :], BLK.bit_length() - 1, None, ALU.arith_shift_right))
            link(v.tensor_copy(cnt[:, :], cntj[:, :]))
            link(v.tensor_scalar(cum[0][:, :], cnt[:, :], 1.0, None, ALU.max))
            link(v.tensor_copy(m.table[:, 0:E], cum[0][0:1, :]))
            for i, s in enumerate((1, 2, 4)):
                v.tensor_copy(cum[i + 1][:, 0:s], cum[i][:, 0:s])
                link(v.tensor_tensor(cum[i + 1][:, s:], cum[i][:, s:], cum[i][:, :E - s], ALU.add))
            link(v.tensor_tensor(base[:, :], cum[3][:, :], cum[0][:, :], ALU.subtract))
            link(v.tensor_copy(m.table[:, E:2 * E], base[0:1, :]))
            link(v.tensor_tensor(rt0[:, :, :], tot[4][:, :, :], tot[0][:, :, :], ALU.subtract))
            link(v.tensor_tensor(rt0[:, :, :], rt0[:, :, :], prank[:, 0:NT * E].rearrange("p (t e) -> p t e", e=E), ALU.add))
            link(v.tensor_scalar(base[:, :], base[:, :], float(BLK), None, ALU.mult))
            link(v.tensor_tensor(rt0[:, :, :], rt0[:, :, :], base[:, :].unsqueeze(1).broadcast_to([P, NT, E]), ALU.add))
            for M, s in ((M1, m.slot1), (M2, m.slot2)):
                link(v.tensor_tensor(rt1[:, :, :], M[:, :, :], rt0[:, :, :], ALU.mult))
                link(v.tensor_reduce(slotf[:, :], rt1[:, :, :], axis=AX.X, op=ALU.add))
                v.tensor_copy(s[:, :], slotf[:, :]).then_inc(slots_made, 1)
                dve.wait_ge(slots_made, 1 if s is m.slot1 else 2)
            for n in range(NT // 2):
                dve.wait_ge(hi_made, n + 1)
                v.tensor_tensor(rows[:, 2 * n:2 * n + 2, D:2 * D], pt[2 + n % 2][:, :].rearrange("p (t d) -> p t d", t=2),
                                rows[:, 2 * n:2 * n + 2, 0:D], ALU.subtract).then_inc(rows_made, 1)
            for n, (lo, full, hi) in enumerate(((m.w1l[0], m.w1f[0], m.w1h[0]), (m.w2l[0], m.w2f[0], m.w2h[0]))):
                dve.wait_ge(first_hi, n + 1)
                v.scalar_tensor_tensor(out=lo[:, :, :], in0=full[:, :, :], scalar=WS, in1=hi[:, :, :], op0=ALU.mult, op1=ALU.subtract)
            lows1(dve)

        @block.tensor
        def _(pe):
            t_ = nc.tensor
            pe.wait_ge(consts, 2)
            pe.wait_ge(small_in, SMALL)
            pe.wait_ge(sty_sb, 1)
            t_.matmul(psty[0:SE, 0:B], emb[:, :], onehot[:, :], start=True, stop=True).then_inc(sty_ps, 1)
            pe.wait_ge(sty_sb, 2)
            t_.matmul(psty[:, B:2 * B], hw1[:, :], st_a[0:SE, :], start=True, stop=True).then_inc(sty_ps, 1)
            pe.wait_ge(sty_sb, 3)
            t_.matmul(psty[:, 2 * B:3 * B], hw2[:, :], st_b[:, :], start=True, stop=True).then_inc(sty_ps, 1)
            pe.wait_ge(sty_sb, 4)
            t_.matmul(psty[0:SH // 2, 3 * B:4 * B], sw1[:, :], st_c[:, :], start=True, stop=True).then_inc(sty_ps, 1)
            pe.wait_ge(sty_sb, 5)
            for i in range(2 * KD):
                last = t_.matmul(psty[:, 16 + i * B:16 + (i + 1) * B], sw2[:, i * P:(i + 1) * P], st_d[0:SH // 2, :], start=True, stop=True)
            last.then_inc(sty_ps, 1)
            for n in range(KD * B):
                k, b = n % KD, n // KD
                pe.wait_ge(z_made, (b + 1) * TPB)
                if n >= 2:
                    pe.wait_ge(hT_made, n - 1)
                for t in range(TPB):
                    last = t_.transpose(pt[n % 2][:, t * P:(t + 1) * P], z[:, b * TPB + t, k * P:(k + 1) * P], m.ident[:, :])
                last.then_inc(zT_made, 1)
            for t in range(NT):
                pe.wait_ge(hmod_made, KD * (t // TPB + 1))
                for k in range(KD):
                    last = t_.matmul(plog[:, t * E:(t + 1) * E], hT[:, k, t * P:(t + 1) * P], rw[:, k, :], start=(k == 0), stop=(k == KD - 1))
            last.then_inc(logits, 1)
            for n in range(NT // 2):
                if n == 2:
                    pe.wait_ge(onehots, 1)
                    t_.matmul(prank[:, 0:NT * E], upper[:, :], Mb[:, :, :].rearrange("p t e -> p (t e)"), start=True, stop=True).then_inc(ranks, 1)
                    t_.matmul(ptot[:, 0:NT * E], ones16[:, :], Mb[:, :, :].rearrange("p t e -> p (t e)"), start=True, stop=True).then_inc(ranks, 1)
                pe.wait_ge(hmod_made, KD * (2 * n // TPB + 1))
                if n >= 2:
                    pe.wait_ge(rows_made, n - 1)
                for j in range(2):
                    for k in range(KD):
                        tok = (2 * n + j) * P
                        last = t_.transpose(pt[2 + n % 2][:, (j * KD + k) * P:(j * KD + k + 1) * P], hT[:, k, tok:tok + P], m.ident[:, :])
                last.then_inc(hback_made, 1)


def experts(nc, a, m):
    with ExitStack() as c:
        def sb(name, shape, dt=F32):
            return c.enter_context(nc.sbuf_tensor(name, shape, dt))

        def ps(name, shape, dt=F32):
            return c.enter_context(nc.psum_tensor(name, shape, dt))

        def sem(name):
            return c.enter_context(nc.semaphore(name))

        HB = BLK // P
        w1f, w2f, w1h, w1l, w2h, w2l = m.w1f, m.w2f, m.w1h, m.w1l, m.w2h, m.w2l
        xin = sb("xin", [P, HB, 2 * D], F16)
        xT = sb("xT", [P, 2 * KD, BLK], F16)
        hh, hl = sb("hh", [P, FC, BLK], F16), sb("hl", [P, FC, BLK], F16)
        yo = sb("yo", [P, HB, D])
        hid = ps("hid", [P, FC, BLK])
        pxT = ps("pxT", [P, 2 * KD, BLK], F16)
        py = ps("py", [P, HB, 512])

        w_hi, w_lo = sem("w_hi"), sem("w_lo")
        w1_in = [sem(f"w1_in{i}") for i in range(2)]
        w2_in = [sem(f"w2_in{i}") for i in range(2)]
        x_loaded, xT_ps, xT_ready = sem("x_loaded"), sem("xT_ps"), sem("xT_ready")
        hid_ps, hid_hi, hid_lo = sem("hid_ps"), sem("hid_hi"), sem("hid_lo")
        y_ps, y_out, y_stored, all_stored = sem("y_ps"), sem("y_out"), sem("y_stored"), sem("all_stored")
        block = c.enter_context(nc.Block())
        xs_v = m.xs.rearrange("(g p) d -> p g d", p=P)
        ys_v = m.ys.rearrange("(g p) d -> p g d", p=P)
        w1_v = a["L0_cond_exp_w1"].rearrange("e (k p) f -> p e k f", p=P)
        w2_v = a["L0_cond_exp_w2"].rearrange("e (k p) d -> p e k d", p=P)

        def each_expert(eng, body):
            def one(i, j, last):
                e = i * 2 + j
                nb = eng.value_load(m.table[0:1, bass.ds(e, 1)], min_val=1, max_val=N // BLK)
                g0 = eng.value_load(m.table[0:1, bass.ds(E + e, 1)], min_val=0, max_val=MAXBLK)
                body(e, i, j, g0, nb, last)
            with eng.Fori(0, E // 2 - 1) as i:
                for j in range(2):
                    one(i, j, False)
            for j in range(2):
                one(E // 2 - 1, j, j == 1)

        @block.gpsimd
        def _(pool):
            def load(e, j):
                pool.dma_start(w1f[j][:, :, :], w1_v[:, bass.ds(e, 1), :, :].squeeze(1)).then_inc(w1_in[j], 16)
                pool.dma_start(w2f[j][:, :, :], w2_v[:, bass.ds(e, 1), :, :].squeeze(1)).then_inc(w2_in[j], 16)
            load(1, 1)
            load(2, 0)
            with pool.Fori(1, E // 2 - 1) as i:
                for j in range(2):
                    pool.wait_ge(w_lo, (i * 2 + j) * 2 - 2 + CREDIT)
                    load(i * 2 + 1 + j, 1 - j)
            pool.wait_ge(w_lo, 2 * (E - 3) + CREDIT)
            load(E - 1, 1)

        @block.sync
        def _(sp):
            sp.sem_inc(y_stored, CREDIT)
            sp.dma_start(xin[:, :, :], xs_v[:, 0:HB, :]).then_inc(x_loaded, 16)
            sp.wait_ge(xT_ps, 1)
            sp.dma_start(xin[:, :, :], xs_v[:, HB:2 * HB, :]).then_inc(x_loaded, 16)

            def body(e, i, j, g0, nb, last):
                with sp.Fori(0, nb) as t:
                    g = sp.snap(g0 + t)
                    sp.wait_ge(xT_ps, g + 2)
                    sp.dma_start(xin[:, :, :], xs_v[:, bass.ds((g + 2) * HB, HB), :]).then_inc(x_loaded, 16)
                    sp.wait_ge(y_out, g + 1 + CREDIT)
                    sp.dma_start(ys_v[:, bass.ds(g * HB, HB), :], yo[:, :, :]).then_inc(y_stored, 16)
                if last:
                    sp.wait_ge(x_loaded, (g0 + nb) * 16 + 32)
                    sp.sem_inc(all_stored, 1)
                    sp.wait_ge(y_stored, (g0 + nb) * 16 + CREDIT)
                    sp.sem_inc(all_stored, 1)
            each_expert(sp, body)

        @block.scalar
        def _(act):
            act.sem_inc(y_out, CREDIT)
            def split(i, j):
                act.wait_ge(w1_in[j], 16 * (i + j))
                nc.scalar.activation(w1h[j][:, :, :], w1f[j][:, :, :], ACT.Copy, scale=WS).then_inc(w_hi, 1)
                act.wait_ge(w2_in[j], 16 * (i + j))
                nc.scalar.activation(w2h[j][:, :, :], w2f[j][:, :, :], ACT.Copy, scale=WS).then_inc(w_hi, 1)

            def body(e, i, j, g0, nb, last):
                def one_block(g, first):
                    for h in range(2):
                        act.wait_ge(hid_ps, g * 2 + h + 1)
                        if h == 0:
                            act.wait_ge(y_ps, g + CREDIT)
                        s = slice(h * FC // 2, (h + 1) * FC // 2)
                        nc.scalar.activation(hh[:, s, :], hid[:, s, :], ACT.Relu).then_inc(hid_hi, 1)
                    if first and not last:
                        act.wait_ge(y_ps, g0 + CREDIT)
                        split(i + j, 1 - j)
                    act.wait_ge(y_ps, g + 1 + CREDIT)
                    act.wait_ge(y_stored, g * 16 + CREDIT)
                    nc.scalar.activation(yo[:, :, :], py[:, :, 0:D], ACT.Copy).then_inc(y_out, 1)
                one_block(g0, True)
                with act.If(nb > 1):
                    with act.Fori(1, nb) as t:
                        one_block(act.snap(g0 + t), False)
            each_expert(act, body)

        @block.vector
        def _(dve):
            dve.sem_inc(hid_lo, CREDIT)
            dve.sem_inc(w_lo, CREDIT)
            v = nc.vector

            def split(e, j):
                dve.wait_ge(w_hi, e * 2 - 1)
                v.scalar_tensor_tensor(out=w1l[j][:, :, :], in0=w1f[j][:, :, :], scalar=WS, in1=w1h[j][:, :, :],
                                       op0=ALU.mult, op1=ALU.subtract).then_inc(w_lo, 1)
                dve.wait_ge(w_hi, e * 2)
                v.scalar_tensor_tensor(out=w2l[j][:, :, :], in0=w2f[j][:, :, :], scalar=WS, in1=w2h[j][:, :, :],
                                       op0=ALU.mult, op1=ALU.subtract).then_inc(w_lo, 1)

            def x_out(g):
                dve.wait_ge(xT_ps, g + 1)
                v.tensor_copy(xT[:, :, :], pxT[:, :, :]).then_inc(xT_ready, 1)
            x_out(0)

            def body(e, i, j, g0, nb, last):
                def one_block(g, first):
                    for h in range(2):
                        dve.wait_ge(hid_hi, g * 2 + h + 1)
                        s = slice(h * FC // 2, (h + 1) * FC // 2)
                        v.scalar_tensor_tensor(out=hl[:, s, :], in0=hid[:, s, :], scalar=0.0, in1=hh[:, s, :],
                                               op0=ALU.max, op1=ALU.subtract).then_inc(hid_lo, 1)
                    dve.wait_ge(hid_ps, g * 2 + 2)
                    x_out(g + 1)
                    if first and not last:
                        split(e + 1, 1 - j)
                one_block(g0, True)
                with dve.If(nb > 1):
                    with dve.Fori(1, nb) as t:
                        one_block(dve.snap(g0 + t), False)
            each_expert(dve, body)

        @block.tensor
        def _(pe):
            pe.sem_inc(y_ps, CREDIT)
            t_ = nc.tensor

            def transposes(g):
                pe.wait_ge(x_loaded, g * 16 + 16)
                pe.wait_ge(xT_ready, g)
                for hb in range(HB):
                    for k in range(2 * KD):
                        last = t_.transpose(pxT[:, k, hb * P:(hb + 1) * P], xin[:, hb, k * P:(k + 1) * P], m.ident16[:, :])
                last.then_inc(xT_ps, 1)
            transposes(0)

            def body(e, i, j, g0, nb, last_expert):
                with pe.Fori(0, nb) as t:
                    g = pe.snap(g0 + t)
                    pe.wait_ge(w_lo, e * 2 + CREDIT)
                    pe.wait_ge(xT_ready, g + 1)
                    for h in range(2):
                        pe.wait_ge(hid_lo, g * 2 + CREDIT)
                        for ch in range(h * FC // 2, (h + 1) * FC // 2):
                            f = slice(ch * P, (ch + 1) * P)
                            t_.matmul(hid[:, ch, :], m.b1row[:, bass.ds(e * FF + ch * P, P)], m.ones16[:, 0:BLK], start=True, stop=False)
                            for k in range(KD):
                                t_.matmul(hid[:, ch, :], w1h[j][:, k, f], xT[:, k, :], start=False, stop=False)
                                t_.matmul(hid[:, ch, :], w1h[j][:, k, f], xT[:, KD + k, :], start=False, stop=False)
                                last = t_.matmul(hid[:, ch, :], w1l[j][:, k, f], xT[:, k, :], start=False, stop=(k == KD - 1))
                        last.then_inc(hid_ps, 1)
                    transposes(g + 1)
                    pe.wait_ge(y_out, g + CREDIT)
                    for h in range(2):
                        pe.wait_ge(hid_lo, g * 2 + h + 1 + CREDIT)
                        for hb in range(HB):
                            tok = slice(hb * P, (hb + 1) * P)
                            if h == 0:
                                t_.matmul(py[:, hb, 0:D], m.ones16[:, 0:P], m.b2row[:, bass.ds(e * D, D)], start=True, stop=False)
                            for ch in range(h * FC // 2, (h + 1) * FC // 2):
                                t_.matmul(py[:, hb, 0:D], hh[:, ch, tok], w2h[j][:, ch, :], start=False, stop=False)
                                t_.matmul(py[:, hb, 0:D], hh[:, ch, tok], w2l[j][:, ch, :], start=False, stop=False)
                                last = t_.matmul(py[:, hb, 0:D], hl[:, ch, tok], w2h[j][:, ch, :], start=False, stop=(ch == FC - 1))
                    last.then_inc(y_ps, 1)
            each_expert(pe, body)


def layer0(nc, a, m):
    with ExitStack() as c:
        m.table = c.enter_context(nc.sbuf_tensor("table", [1, 2 * E], I32))
        m.b1row = c.enter_context(nc.sbuf_tensor("b1row", [P, E * FF], F16))
        m.b2row = c.enter_context(nc.sbuf_tensor("b2row", [P, E * D], F16))
        two = lambda name, shape, dt: [c.enter_context(nc.sbuf_tensor(f"{name}{i}", shape, dt)) for i in range(2)]
        m.w1f, m.w2f = two("w1f", [P, KD, FF], F32), two("w2f", [P, FC, D], F32)
        m.w1h, m.w1l = two("w1h", [P, KD, FF], F16), two("w1l", [P, KD, FF], F16)
        m.w2h, m.w2l = two("w2h", [P, FC, D], F16), two("w2l", [P, FC, D], F16)
        m.first_w = [c.enter_context(nc.semaphore(f"first_w{i}")) for i in range(2)]
        front(nc, a, m)
        experts(nc, a, m)


def norm_transpose(nc, m, src, gamma, beta, name):
    with ExitStack() as c:
        def sb(name_, shape, dt=F32):
            return c.enter_context(nc.sbuf_tensor(name + name_, shape, dt))

        def sem(name_):
            return c.enter_context(nc.semaphore(name + name_))

        z = sb("z", [P, NT, D])
        stats, mv, rstd = sb("stats", [P, NT, 6]), sb("mv", [P, NT, 2]), sb("rstd", [P, NT])
        full = [sb(f"full{i}", [P, T]) for i in range(2)]
        pt = [c.enter_context(nc.psum_tensor(f"{name}pt{i}", [P, T], F32)) for i in range(2)]
        st_made, var_made, eps_made, rstd_made = sem("st_made"), sem("var_made"), sem("eps_made"), sem("rstd_made")
        z_made, zT_made, full_made, hi_made, lo_made = sem("z_made"), sem("zT_made"), sem("full_made"), sem("hi_made"), sem("lo_made")
        block = c.enter_context(nc.Block())

        @block.gpsimd
        def _(pool):
            for b in range(B):
                r = rstd[:, b * TPB:(b + 1) * TPB]
                pool.wait_ge(var_made, b + 1)
                nc.gpsimd.tensor_scalar(r, mv[:, b * TPB:(b + 1) * TPB, 1], 1e-5, None, ALU.add).then_inc(eps_made, 1)
                pool.wait_ge(eps_made, b + 1)
                nc.gpsimd.tensor_tensor(r, r, m.mhalf[:, 0:TPB], ALU.pow).then_inc(rstd_made, 1)

        @block.scalar
        def _(act):
            for n in range(KD * B):
                k, b = n % KD, n // KD
                act.wait_ge(zT_made, n + 1)
                if n >= 2:
                    act.wait_ge(lo_made, n - 1)
                nc.scalar.activation(full[n % 2][:, :], pt[n % 2][:, :], ACT.Identity,
                                     bias=beta[:, k:k + 1], scale=gamma[:, k:k + 1]).then_inc(full_made, 1)

        @block.vector
        def _(dve):
            v = nc.vector

            def statistics(b):
                for t in range(b * TPB, (b + 1) * TPB):
                    last = v.bn_stats(out=stats[:, t, :], in_=src[:, t, :])
                last.then_inc(st_made, 1)
                dve.wait_ge(st_made, b + 1)
                for t in range(b * TPB, (b + 1) * TPB):
                    last = v.bn_aggr(out=mv[:, t, :], in_=stats[:, t, :])
                last.then_inc(var_made, 1)
            statistics(0)
            for b in range(B):
                if b + 1 < B:
                    statistics(b + 1)
                dve.wait_ge(rstd_made, b + 1)
                for t in range(b * TPB, (b + 1) * TPB):
                    v.tensor_scalar(z[:, t, :], src[:, t, :], mv[:, t, 0:1], rstd[:, t:t + 1],
                                    ALU.subtract, ALU.mult).then_inc(z_made, 1)
            for n in range(KD * B):
                k, b = n % KD, n // KD
                tok = slice(b * T, (b + 1) * T)
                dve.wait_ge(full_made, n + 1)
                v.tensor_copy(m.hTh[:, k, tok], full[n % 2][:, :]).then_inc(hi_made, 1)
                dve.wait_ge(hi_made, n + 1)
                v.tensor_tensor(m.hTl[:, k, tok], full[n % 2][:, :], m.hTh[:, k, tok], ALU.subtract).then_inc(lo_made, 1)

        @block.tensor
        def _(pe):
            for n in range(KD * B):
                k, b = n % KD, n // KD
                pe.wait_ge(z_made, (b + 1) * TPB)
                if n >= 2:
                    pe.wait_ge(full_made, n - 1)
                for t in range(TPB):
                    last = nc.tensor.transpose(pt[n % 2][:, t * P:(t + 1) * P], z[:, b * TPB + t, k * P:(k + 1) * P], m.ident[:, :])
                last.then_inc(zT_made, 1)


def attention(nc, m):
    with ExitStack() as c:
        def sb(name, shape, dt=F32):
            return c.enter_context(nc.sbuf_tensor(name, shape, dt))

        def ps(name, shape, dt=F32):
            return c.enter_context(nc.psum_tensor(name, shape, dt))

        def sem(name):
            return c.enter_context(nc.semaphore(name))

        qa, qb = [sb(f"qa{i}", [P, T], F16) for i in range(2)], [sb(f"qb{i}", [P, T], F16) for i in range(2)]
        ka, kb = [sb(f"ka{i}", [P, T], F16) for i in range(2)], [sb(f"kb{i}", [P, T], F16) for i in range(2)]
        qs, kl = sb("qs", [P, T], F16), sb("kl", [P, T], F16)
        pT = [sb(f"pT{i}", [P, TPB, HG, T]) for i in range(2)]
        mx, rc = sb("mx", [P, TPB, HG]), sb("rc", [P, TPB, HG])
        cT = sb("cT", [P, T])
        pS = [ps(f"pS{i}", [P, 2, T]) for i in range(2)]
        pM = [ps(f"pM{i}", [P, T]) for i in range(2)]
        pA, pB = ps("pA", [P, T]), ps("pB", [P, T])
        y1, y2 = sb("y1", [P, TPB, D]), sb("y2", [P, TPB, D])
        slots = [sb(f"slots{i}", [P, TPB], U32) for i in range(2)]
        z, full = sb("z1", [P, TPB, D]), [sb(f"full{i}", [P, T]) for i in range(2)]
        stats, mv, rstd = sb("stats1", [P, TPB, 6]), sb("mv1", [P, TPB, 2]), sb("rstd1", [P, TPB])

        slots_here, got = sem("slots_here"), [sem(f"got_{t}") for t in range(TPB)]
        half, summed = sem("half"), sem("summed")
        st_made, var_made, eps_made, rstd_made = sem("st1_made"), sem("var1_made"), sem("eps1_made"), sem("rstd1_made")
        dve_seen, pool_seen = sem("dve_seen"), sem("pool_seen")
        z_made, zT_ps, full_made, h_hi, h_lo = sem("z1_made"), sem("zT_ps"), sem("full_made"), sem("h_hi"), sem("h_lo")
        q_ps, k_ps, qs_made, qa_made = sem("q_ps"), sem("k_ps"), sem("qs_made"), sem("qa_made")
        ka_made, kl_made, kb_made = sem("ka_made"), sem("kl_made"), sem("kb_made")
        s_ps, exp_made, exp_seen, masked = sem("s_ps"), sem("exp_made"), sem("exp_seen"), sem("masked")
        mx_ps, mx_made, nmh_made, nm_made, nmT_ps, qb_made = sem("mx_ps"), sem("mx_made"), sem("nmh_made"), sem("nm_made"), sem("nmT_ps"), sem("qb_made")
        v_ps, v_made = sem("v_ps"), sem("v_made")
        ctx_ps, ctx_sb, ctxT_ps, rc_made, ctx_made = sem("ctx_ps"), sem("ctx_sb"), sem("ctxT_ps"), sem("rc_made"), sem("ctx_made")
        block = c.enter_context(nc.Block())
        UNITS = [(hp, t) for hp in range(2) for t in range(TPB)]
        NU = len(UNITS)

        def batches(eng, body):
            with eng.Fori(0, B - 1) as b:
                body(b, False)
            body(B - 1, True)

        def nxt(b, g, d):
            return b + (g + d) // G, (g + d) % G

        @block.tensor
        def _(pe):
            pe.sem_inc(ctxT_ps, CREDIT)
            t_ = nc.tensor

            def project(b, g, pk=pB[:, :], pq=pA[:, :]):
                gs = slice(g * P, (g + 1) * P)
                for (wh, wl), out, n, ready in ((m.wk, pk, 1, k_ps), (m.wq, pq, 0, q_ps)):
                    t_.matmul(out, m.bdup[:, n, gs], m.ones16[:, :], start=True, stop=False)
                    for k in range(KD):
                        xh, xl = m.hTh[:, k, bass.ds(b * T, T)], m.hTl[:, k, bass.ds(b * T, T)]
                        t_.matmul(out, wh[:, k, gs], xh, start=False, stop=False)
                        t_.matmul(out, wh[:, k, gs], xl, start=False, stop=False)
                        last = t_.matmul(out, wl[:, k, gs], xh, start=False, stop=(k == KD - 1))
                    last.then_inc(ready, 1)

            def norm_transposed(b, k, out):
                for t in range(TPB):
                    last = t_.transpose(out[:, t * P:(t + 1) * P], z[:, t, k * P:(k + 1) * P], m.ident[:, :])
                last.then_inc(zT_ps, 1)

            def values(b):
                for n in range(TPB // 2):
                    for j in range(2):
                        out = pS[0][:, n, j * D:(j + 1) * D]
                        t_.matmul(out, m.ones16[:, 0:P], m.brow[:, 2, :], start=True, stop=False)
                        for k in range(KD):
                            tok = bass.ds(b * T + (2 * n + j) * P, P)
                            t_.matmul(out, m.hTh[:, k, tok], m.wv[0][:, k, :], start=False, stop=False)
                            t_.matmul(out, m.hTl[:, k, tok], m.wv[0][:, k, :], start=False, stop=False)
                            last = t_.matmul(out, m.hTh[:, k, tok], m.wv[1][:, k, :], start=False, stop=(k == KD - 1))
                    last.then_inc(v_ps, 1)

            def max_unit(b, g, u):
                i = b * G + g
                hp, qt = UNITS[u]
                p = g % 2
                n = (qt + 1) * P
                for j in range(2):
                    if u or j:
                        pe.wait_ge(mx_made, 2 * (i * NU + u) + j - 1)
                    t_.matmul(pM[j][:, qt * P:n], m.identb[:, :], m.future[:, :], start=True, stop=True)
                    r = slice((2 * hp + j) * Q32, (2 * hp + j + 1) * Q32)
                    t_.matmul(pM[j][:, 0:n], qa[p][r, qt * P:n], ka[p][r, 0:n], start=False, stop=True,
                              skip_group_check=True).then_inc(mx_ps, 1)

            def max_transposed(b, g):
                i = b * G + g
                pe.wait_ge(nm_made, i + 1)
                for qt in range(TPB):
                    last = t_.transpose(pM[0][:, :].bitcast(F16)[:, qt * P:(qt + 1) * P], m.nmp[:, qt, :], m.ident16[:, :])
                last.then_inc(nmT_ps, 1)

            def score_unit(b, g, u):
                i = b * G + g
                hp, kt = UNITS[u]
                p = g % 2
                k0 = kt * P
                pe.wait_ge(exp_made, i * NU + (u - 1 if u else 0) + CREDIT)
                for kk, qq, start in ((ka, qa, True), (kb, qb, False)):
                    for j in range(2):
                        r = slice((2 * hp + j) * Q32, (2 * hp + j + 1) * Q32)
                        last = t_.matmul(pS[u % 2][:, j, k0:T], kk[p][r, k0:k0 + P], qq[p][r, k0:T], start=start, stop=not start)
                last.then_inc(s_ps, 1)

            def weighted(b, g):
                i = b * G + g
                pe.wait_ge(masked, (i + 1) * NU)
                for kt in range(TPB):
                    for j in range(HG):
                        last = t_.matmul(pB[j * Q32:(j + 1) * Q32, kt * P:T], m.vp[:, kt, g * HG + j, :],
                                         pT[g % 2][:, kt, j, kt * P:T], start=(kt == 0), stop=(kt == TPB - 1))
                last.then_inc(ctx_ps, 1)

            def context_transposed(i):
                pe.wait_ge(ctx_sb, i + 1 + CREDIT)
                for qt in range(TPB):
                    last = t_.transpose(pA[:, qt * P:(qt + 1) * P], cT[:, qt * P:(qt + 1) * P], m.ident[:, :])
                last.then_inc(ctxT_ps, 1)

            pe.wait_ge(z_made, TPB)
            norm_transposed(0, 0, pA)
            norm_transposed(0, 1, pB)
            pe.wait_ge(h_lo, KD)
            project(0, 0)
            values(0)
            project(0, 1, pS[1][:, 0, :], pS[1][:, 1, :])
            pe.wait_ge(qa_made, 1)
            for u in range(NU):
                max_unit(0, 0, u)
            pe.wait_ge(qa_made, 2)
            max_transposed(0, 0)

            def body(b, last_batch):
                for g in range(G):
                    i = b * G + g
                    n1, n2 = not (last_batch and g == G - 1), not (last_batch and g >= G - 2)
                    pe.wait_ge(qb_made, i + 1)
                    if n1:
                        pe.wait_ge(kb_made, i + 2)
                    for u in range(NU):
                        if g == 0 and u == 0:
                            pe.wait_ge(v_made, (b + 1) * (TPB // 2))
                        score_unit(b, g, u)
                        if n1:
                            max_unit(*nxt(b, g, 1), u)
                        if u == 2 and g:
                            context_transposed(i - 1)
                        if g == 1 and not last_batch and u >= NU - KD:
                            k = u - (NU - KD)
                            pe.wait_ge(z_made, (b + 2) * TPB)
                            if k:
                                pe.wait_ge(full_made, (b + 1) * KD + k)
                            else:
                                pe.wait_ge(ctx_made, i + CREDIT)
                            norm_transposed(b + 1, k, pA)
                    pe.wait_ge(ctx_sb, i + CREDIT)
                    if n2:
                        pe.wait_ge(ctx_made, i + CREDIT)
                        if g == 1 and not last_batch:
                            pe.wait_ge(full_made, (b + 2) * KD)
                        if g == 2:
                            pe.wait_ge(h_lo, (b + 2) * KD)
                        project(*nxt(b, g, 2))
                    if n1:
                        max_transposed(*nxt(b, g, 1))
                    if n2:
                        pe.wait_ge(kl_made, i + 3)
                    weighted(b, g)
                    if g == G - 1 and not last_batch:
                        values(b + 1)
                        pe.wait_ge(qa_made, i + 3)
                    if g == G - 1:
                        pe.wait_ge(ctx_made, i + CREDIT)
                        context_transposed(i)
            batches(pe, body)

        @block.scalar
        def _(act):
            act.sem_inc(exp_made, CREDIT)
            act.sem_inc(ctx_sb, CREDIT)
            s_ = nc.scalar

            def projected(b, g, pk=pB[:, :], pq=pA[:, :]):
                i = b * G + g
                act.wait_ge(k_ps, i + 1)
                s_.activation(ka[g % 2][:, :], pk, ACT.Copy).then_inc(ka_made, 1)
                act.wait_ge(q_ps, i + 1)
                act.wait_ge(qa_made, i)
                s_.activation(qs[:, :], pq, ACT.Copy, scale=m.msign[:, 0:1]).then_inc(qs_made, 1)

            def values(b):
                for n in range(TPB // 2):
                    act.wait_ge(v_ps, b * (TPB // 2) + n + 1)
                    s_.activation(m.vp[:, 2 * n:2 * n + 2, :, 0:HD],
                                  pS[0][:, n, :].rearrange("p (t h d) -> p t h d", t=2, d=HD), ACT.Copy, scale=1.0 / WS).then_inc(v_made, 1)
            def norm_scaled(b, k, src):
                act.wait_ge(zT_ps, b * KD + k + 1)
                s_.activation(full[k][:, :], src[:, :], ACT.Identity, bias=m.be1[:, k:k + 1], scale=m.g1[:, k:k + 1]).then_inc(full_made, 1)

            norm_scaled(0, 0, pA)
            norm_scaled(0, 1, pB)
            projected(0, 0)
            values(0)
            projected(0, 1, pS[1][:, 0, :], pS[1][:, 1, :])

            def body(b, last_batch):
                for g in range(G):
                    i = b * G + g
                    for u, (hp, kt) in enumerate(UNITS):
                        act.wait_ge(s_ps, i * NU + u + 1)
                        s_.activation(pT[g % 2][:, kt, 2 * hp:2 * hp + 2, kt * P:T], pS[u % 2][:, :, kt * P:T],
                                      ACT.Exp, scale=HD ** -0.5 / MS).then_inc(exp_made, 1)
                        if g == 1 and not last_batch and u >= NU - KD:
                            k = u - (NU - KD)
                            act.wait_ge(h_lo, (b + 1) * KD)
                            norm_scaled(b + 1, k, pA)
                    if not (last_batch and g >= G - 2):
                        projected(*nxt(b, g, 2))
                    act.wait_ge(ctx_ps, i + 1)
                    act.wait_ge(ctxT_ps, i + CREDIT)
                    s_.activation(cT[:, :], pB[:, :], ACT.Copy).then_inc(ctx_sb, 1)
                    if g == G - 1 and not last_batch:
                        values(b + 1)
            batches(act, body)

        @block.vector
        def _(dve):
            dve.sem_inc(ctx_made, CREDIT)
            v = nc.vector

            def projected(b, g, pk=pB[:, :], pq=pA[:, :]):
                i = b * G + g
                p = g % 2
                dve.wait_ge(ka_made, i + 1)
                v.tensor_tensor(kl[:, :], pk, ka[p][:, :], ALU.subtract).then_inc(kl_made, 1)
                dve.wait_ge(kl_made, i + 1)
                v.tensor_scalar(kb[p][:, :], kl[:, :], m.mfirst[:, 0:1], m.kconst[:, 0:1], ALU.mult, ALU.add).then_inc(kb_made, 1)
                dve.wait_ge(qs_made, i + 1)
                v.scalar_tensor_tensor(out=qa[p][:, :], in0=pq, scalar=m.mlow[:, 0:1], in1=qs[:, :],
                                       op0=ALU.mult, op1=ALU.add).then_inc(qa_made, 1)

            def maximum(b, g, u):
                i = b * G + g
                hp, qt = UNITS[u]
                for j in range(2):
                    dve.wait_ge(mx_ps, 2 * (i * NU + u) + j + 1)
                    v.tensor_reduce(mx[:, qt, 2 * hp + j:2 * hp + j + 1], pM[j][:, 0:(qt + 1) * P], axis=AX.X, op=ALU.max).then_inc(mx_made, 1)

            def negated(b, g):
                i = b * G + g
                dve.wait_ge(mx_made, 2 * (i + 1) * NU)
                dve.wait_ge(nmT_ps, i)
                hi = m.nmp[:, :, :].rearrange("p t (h r) -> p t h r", r=Q32)[:, :, :, HD]
                lo = m.nmp[:, :, :].rearrange("p t (h r) -> p t h r", r=Q32)[:, :, :, HD + 1]
                v.tensor_scalar(hi, mx[:, :, :], -1.0 / MS, None, ALU.mult).then_inc(nmh_made, 1)
                dve.wait_ge(nmh_made, i + 1)
                v.scalar_tensor_tensor(out=lo, in0=mx[:, :, :], scalar=-1.0 / MS, in1=hi, op0=ALU.mult, op1=ALU.subtract).then_inc(nm_made, 1)

            def queries_b(b, g):
                i = b * G + g
                dve.wait_ge(nmT_ps, i + 1)
                dve.wait_ge(qa_made, i + 1)
                v.scalar_tensor_tensor(out=qb[g % 2][:, :], in0=qa[g % 2][:, :], scalar=m.mfirst[:, 0:1],
                                       in1=pM[0][:, :].bitcast(F16)[:, 0:T], op0=ALU.mult, op1=ALU.add).then_inc(qb_made, 1)

            def context(b, g):
                i = b * G + g
                dve.wait_ge(ctxT_ps, i + 1 + CREDIT)
                o = pA[:, :].rearrange("p (t h r) -> p t h r", t=TPB, r=Q32)
                v.reciprocal(rc[:, :, :], o[:, :, :, HD]).then_inc(rc_made, 1)
                dve.wait_ge(rc_made, i + 1)
                v.tensor_tensor(m.ctx[:, bass.ds(b * TPB, TPB), g * HG * HD:(g + 1) * HG * HD].rearrange("p t (h d) -> p t h d", d=HD),
                                o[:, :, :, 0:HD], rc[:, :, :].unsqueeze(3).broadcast_to([P, TPB, HG, HD]), ALU.mult).then_inc(ctx_made, 1)

            def summed_rows(b, ts):
                for t in ts:
                    x = m.x[:, bass.ds(b * TPB + t, 1), :].squeeze(1)
                    dve.wait_ge(got[t], 32 * (b + 1))
                    v.scalar_tensor_tensor(out=x, in0=y1[:, t, :], scalar=m.gate1[:, bass.ds(b * TPB + t, 1)], in1=x,
                                           op0=ALU.mult, op1=ALU.add).then_inc(half, 1)
                    dve.wait_ge(half, b * TPB + t + 1)
                    v.scalar_tensor_tensor(out=x, in0=y2[:, t, :], scalar=m.gate2[:, bass.ds(b * TPB + t, 1)], in1=x,
                                           op0=ALU.mult, op1=ALU.add).then_inc(summed, 1)
                    dve.wait_ge(summed, b * TPB + t + 1)
                    dve.sem_inc(dve_seen, 1)
                    v.bn_stats(out=stats[:, t, :], in_=x).then_inc(st_made, 1)

            def aggregated(b):
                dve.wait_ge(st_made, (b + 1) * TPB)
                dve.sem_inc(dve_seen, 1)
                for t in range(TPB):
                    last = v.bn_aggr(out=mv[:, t, :], in_=stats[:, t, :])
                last.then_inc(var_made, 1)

            def standardised(b, ts):
                dve.wait_ge(rstd_made, b + 1)
                for t in ts:
                    v.tensor_scalar(z[:, t, :], m.x[:, bass.ds(b * TPB + t, 1), :].squeeze(1), mv[:, t, 0:1], rstd[:, t:t + 1],
                                    ALU.subtract, ALU.mult).then_inc(z_made, 1)

            def norm_split(b, k):
                hi, lo = m.hTh[:, k, bass.ds(b * T, T)], m.hTl[:, k, bass.ds(b * T, T)]
                dve.wait_ge(full_made, b * KD + k + 1)
                v.tensor_copy(hi, full[k][:, :]).then_inc(h_hi, 1)
                dve.wait_ge(h_hi, b * KD + k + 1)
                v.tensor_tensor(lo, full[k][:, :], hi, ALU.subtract).then_inc(h_lo, 1)

            summed_rows(0, range(TPB))
            aggregated(0)
            standardised(0, range(TPB))
            for k in range(KD):
                norm_split(0, k)
            projected(0, 0)
            dve.wait_ge(kb_made, 1)
            projected(0, 1, pS[1][:, 0, :], pS[1][:, 1, :])
            for u in range(NU):
                maximum(0, 0, u)
            negated(0, 0)
            queries_b(0, 0)

            def body(b, last_batch):
                for g in range(G):
                    n1, n2 = not (last_batch and g == G - 1), not (last_batch and g >= G - 2)
                    for u in range(NU):
                        if n1:
                            maximum(*nxt(b, g, 1), u)
                        if u == 3 and g:
                            context(b, g - 1)
                        if g == 0 and u > NU - TPB and not last_batch:
                            summed_rows(b + 1, (u - 1 - (NU - TPB),))
                        if g == 1 and u < TPB and not last_batch:
                            if u == 0:
                                dve.wait_ge(zT_ps, (b + 1) * KD)
                            standardised(b + 1, (u,))
                    if n1:
                        negated(*nxt(b, g, 1))
                    if g == 1 and not last_batch:
                        for k in range(KD):
                            norm_split(b + 1, k)
                    if n2:
                        projected(*nxt(b, g, 2))
                    if n1:
                        queries_b(*nxt(b, g, 1))
                    if g == 0 and not last_batch:
                        summed_rows(b + 1, (TPB - 1,))
                        aggregated(b + 1)
                    if g == G - 1:
                        context(b, g)
            batches(dve, body)

        @block.gpsimd
        def _(pool):
            def slots_copied(b):
                for n, s in enumerate((m.slot1, m.slot2)):
                    last = nc.gpsimd.tensor_copy(slots[n][:, :], s[:, bass.ds(b * TPB, TPB)])
                last.then_inc(slots_here, 1)

            def gather(b, t, n):
                nc.gpsimd.indirect_dma_start(out=(y1, y2)[n][:, t, :], out_offset=None, in_=m.ys[0:MAXBLK * BLK, :],
                                             in_offset=bass.IndirectOffsetOnAxis(ap=slots[n][:, t:t + 1], axis=0)).then_inc(got[t], 16)

            def deviation(b):
                pool.wait_ge(var_made, b + 1)
                pool.sem_inc(pool_seen, 1)
                nc.gpsimd.tensor_scalar(rstd[:, :], mv[:, :, 1], 1e-5, None, ALU.add).then_inc(eps_made, 1)
                pool.wait_ge(eps_made, b + 1)
                nc.gpsimd.tensor_tensor(rstd[:, :], rstd[:, :], m.mhalf[:, 0:TPB], ALU.pow).then_inc(rstd_made, 1)

            slots_copied(0)
            pool.wait_ge(slots_here, 1)
            for t in range(TPB):
                for n in range(TOPK):
                    gather(0, t, n)
            deviation(0)

            def body(b, last_batch):
                for g in range(G):
                    i = b * G + g
                    if g == 0 and not last_batch:
                        pool.wait_ge(summed, (b + 1) * TPB)
                        slots_copied(b + 1)
                        pool.wait_ge(slots_here, b + 2)
                        pool.sem_inc(pool_seen, 1)
                        for t in range(TPB):
                            for n in range(TOPK):
                                gather(b + 1, t, n)
                    if g == 1 and not last_batch:
                        deviation(b + 1)
                    for u, (hp, kt) in enumerate(UNITS):
                        pool.wait_ge(exp_made, i * NU + u + 1 + CREDIT)
                        pool.sem_inc(exp_seen, 1)
                        d = pT[g % 2][:, kt, 2 * hp:2 * hp + 2, kt * P:(kt + 1) * P]
                        nc.gpsimd.affine_select(out=d, in_=d, compare_op=ALU.is_ge, fill=0.0, base=0,
                                                pattern=[[0, 2], [1, P]], channel_multiplier=-1).then_inc(masked, 1)
            batches(pool, body)


def output_projection(nc, m):
    with ExitStack() as c:
        def sb(name, shape, dt=F32):
            return c.enter_context(nc.sbuf_tensor(name, shape, dt))

        def ps(name, shape, dt=F32):
            return c.enter_context(nc.psum_tensor(name, shape, dt))

        def sem(name):
            return c.enter_context(nc.semaphore(name))

        ch = [sb(f"ch{i}", [P, 2, KD, P], F16) for i in range(2)]
        cl = [sb(f"cl{i}", [P, 2, KD, P], F16) for i in range(2)]
        pt = [ps(f"pto{i}", [P, 2, KD, P]) for i in range(2)]
        po = [ps(f"po{i}", [P, 2, D]) for i in range(2)]
        cT_ps, hi_made, lo_made, o_ps, x1_made = sem("cT_ps"), sem("o_hi"), sem("o_lo"), sem("o_ps"), sem("x1_made")
        block = c.enter_context(nc.Block())
        NP = NT // 2

        @block.tensor
        def _(pe):
            t_ = nc.tensor

            def transposes(n):
                if n >= 2:
                    pe.wait_ge(lo_made, n - 1)
                for j in range(2):
                    for k in range(KD):
                        last = t_.transpose(pt[n % 2][:, j, k, :], m.ctx[:, 2 * n + j, k * P:(k + 1) * P], m.ident[:, :])
                last.then_inc(cT_ps, 1)
            transposes(0)
            for n in range(NP):
                if n + 1 < NP:
                    transposes(n + 1)
                pe.wait_ge(lo_made, n + 1)
                if n >= 2:
                    pe.wait_ge(x1_made, n - 1)
                for j in range(2):
                    out = po[n % 2][:, j, :]
                    t_.matmul(out, m.ones16[:, 0:P], m.brow[:, 3, :], start=True, stop=False)
                    for k in range(KD):
                        t_.matmul(out, ch[n % 2][:, j, k, :], m.wo[0][:, k, :], start=False, stop=False)
                        t_.matmul(out, cl[n % 2][:, j, k, :], m.wo[0][:, k, :], start=False, stop=False)
                        last = t_.matmul(out, ch[n % 2][:, j, k, :], m.wo[1][:, k, :], start=False, stop=(k == KD - 1))
                last.then_inc(o_ps, 1)

        @block.scalar
        def _(act):
            for n in range(NP):
                act.wait_ge(cT_ps, n + 1)
                if n >= 2:
                    act.wait_ge(o_ps, n - 1)
                nc.scalar.activation(ch[n % 2][:, :, :, :], pt[n % 2][:, :, :, :], ACT.Copy).then_inc(hi_made, 1)

        @block.vector
        def _(dve):
            v = nc.vector

            def low(n):
                dve.wait_ge(hi_made, n + 1)
                v.tensor_tensor(cl[n % 2][:, :, :, :].rearrange("p j k q -> p (j k q)"), pt[n % 2][:, :, :, :].rearrange("p j k q -> p (j k q)"),
                                ch[n % 2][:, :, :, :].rearrange("p j k q -> p (j k q)"), ALU.subtract).then_inc(lo_made, 1)
            low(0)
            for n in range(NP):
                if n + 1 < NP:
                    low(n + 1)
                dve.wait_ge(o_ps, n + 1)
                v.scalar_tensor_tensor(out=m.x1[:, 2 * n:2 * n + 2, :], in0=po[n % 2][:, :, :], scalar=1.0 / WS,
                                       in1=m.x[:, 2 * n:2 * n + 2, :], op0=ALU.mult, op1=ALU.add).then_inc(x1_made, 1)


def feed_forward(nc, m, out):
    with ExitStack() as c:
        def sb(name, shape, dt=F32):
            return c.enter_context(nc.sbuf_tensor(name, shape, dt))

        def ps(name, shape, dt=F32):
            return c.enter_context(nc.psum_tensor(name, shape, dt))

        def sem(name):
            return c.enter_context(nc.semaphore(name))

        ge = [sb(f"ge{i}", [P, T]) for i in range(2)]
        gh, gl = sb("gh", [P, FC, T], F16), sb("gl", [P, FC, T], F16)
        o = [sb(f"o{i}", [P, 2, D]) for i in range(2)]
        ph = [ps(f"ph{i}", [P, T]) for i in range(2)]
        py = [ps(f"pyf{i}", [P, 2, D]) for i in range(2)]
        h_ps, ge_made, gh_made, gl_made, y_ps = sem("h_ps"), sem("ge_made"), sem("gh_made"), sem("gl_made"), sem("yf_ps")
        o1, o2, o3 = sem("o1"), sem("o2"), sem("o3")
        stored = [sem(f"stored{i}") for i in range(2)]
        block = c.enter_context(nc.Block())
        NP = TPB // 2
        out_v = out.rearrange("b (t p) d -> p (b t) d", p=P)

        @block.tensor
        def _(pe):
            pe.sem_inc(y_ps, CREDIT)
            t_ = nc.tensor
            with pe.Fori(0, B) as b:
                for ch in range(FC):
                    f = slice(ch * P, (ch + 1) * P)
                    pe.wait_ge(ge_made, b * FC + max(ch - 1, 0) + CREDIT)
                    for k in range(KD):
                        xh, xl = m.hTh[:, k, bass.ds(b * T, T)], m.hTl[:, k, bass.ds(b * T, T)]
                        t_.matmul(ph[ch % 2][:, :], m.f1h[:, k, f], xh, start=(k == 0), stop=False)
                        t_.matmul(ph[ch % 2][:, :], m.f1h[:, k, f], xl, start=False, stop=False)
                        last = t_.matmul(ph[ch % 2][:, :], m.f1l[:, k, f], xh, start=False, stop=(k == KD - 1))
                    last.then_inc(h_ps, 1)
                for n in range(NP):
                    pe.wait_ge(o1, b * NP + max(n - 1, 0) + CREDIT)
                    for j in range(2):
                        y = py[n % 2][:, j, :]
                        tok = slice((2 * n + j) * P, (2 * n + j + 1) * P)
                        t_.matmul(y, m.ones16[:, 0:P], m.brow[:, 4, :], start=True, stop=False)
                        for ch in range(FC):
                            pe.wait_ge(gl_made, b * FC + ch + 1 + CREDIT)
                            t_.matmul(y, gh[:, ch, tok], m.f2h[:, ch, :], start=False, stop=False)
                            t_.matmul(y, gl[:, ch, tok], m.f2h[:, ch, :], start=False, stop=False)
                            last = t_.matmul(y, gh[:, ch, tok], m.f2l[:, ch, :], start=False, stop=(ch == FC - 1))
                    last.then_inc(y_ps, 1)

        @block.scalar
        def _(act):
            act.sem_inc(ge_made, CREDIT)
            with act.Fori(0, B) as b:
                for ch in range(FC):
                    act.wait_ge(h_ps, b * FC + ch + 1)
                    act.wait_ge(gl_made, b * FC + max(ch - 1, 0) + CREDIT)
                    nc.scalar.activation(ge[ch % 2][:, :], ph[ch % 2][:, :], ACT.Gelu, bias=m.bff[:, ch:ch + 1],
                                         scale=1.0 / WS).then_inc(ge_made, 1)

        @block.vector
        def _(dve):
            dve.sem_inc(gl_made, CREDIT)
            dve.sem_inc(o1, CREDIT)
            v = nc.vector
            with dve.Fori(0, B) as b:
                for ch in range(FC):
                    dve.wait_ge(ge_made, b * FC + ch + 1 + CREDIT)
                    if ch == 0:
                        dve.wait_ge(y_ps, b * NP + CREDIT)
                    v.tensor_copy(gh[:, ch, :], ge[ch % 2][:, :]).then_inc(gh_made, 1)
                    dve.wait_ge(gh_made, b * FC + ch + 1)
                    v.tensor_tensor(gl[:, ch, :], ge[ch % 2][:, :], gh[:, ch, :], ALU.subtract).then_inc(gl_made, 1)
                for n in range(NP):
                    dve.wait_ge(y_ps, b * NP + n + 1 + CREDIT)
                    dve.wait_ge(stored[n], b * 16 + CREDIT)
                    ts = bass.ds(b * TPB + 2 * n, 2)
                    v.scalar_tensor_tensor(out=o[n][:, :, :], in0=py[n][:, :, :], scalar=1.0 / WS, in1=m.x1[:, ts, :],
                                           op0=ALU.mult, op1=ALU.add).then_inc(o1, 1)
                    dve.wait_ge(o1, b * NP + n + 1 + CREDIT)
                    v.tensor_tensor(o[n][:, :, :], o[n][:, :, :], m.x[:, ts, :], ALU.subtract).then_inc(o2, 1)
                    dve.wait_ge(o2, b * NP + n + 1)
                    v.scalar_tensor_tensor(out=o[n][:, :, :], in0=o[n][:, :, :], scalar=m.gs[:, bass.ds(b, 1)], in1=m.x[:, ts, :],
                                           op0=ALU.mult, op1=ALU.add).then_inc(o3, 1)

        @block.sync
        def _(sp):
            sp.sem_inc(stored[0], CREDIT)
            sp.sem_inc(stored[1], CREDIT)
            with sp.Fori(0, B) as b:
                for n in range(NP):
                    sp.wait_ge(o3, b * NP + n + 1)
                    sp.dma_start(out_v[:, bass.ds(b * TPB + 2 * n, 2), :], o[n][:, :, :]).then_inc(stored[n], 16)
            for n in range(NP):
                sp.wait_ge(stored[n], 16 * B + CREDIT)


def layer1_tensors(nc, m, c):
    def sb(name, shape, dt=F32):
        return c.enter_context(nc.sbuf_tensor(name, shape, dt))

    pair = lambda name, shape: (sb(name + "h", shape, F16), sb(name + "l", shape, F16))
    m.g1, m.be1, m.g2, m.be2 = sb("g1", [P, KD]), sb("be1", [P, KD]), sb("g2", [P, KD]), sb("be2", [P, KD])
    m.bff, m.gs = sb("bff", [P, FC]), sb("gs", [P, B])
    m.wq, m.wk = pair("wq", [P, KD, 2 * D]), pair("wk", [P, KD, 2 * D])
    m.wv, m.wo = pair("wv", [P, KD, D]), pair("wo", [P, KD, D])
    m.f1h, m.f1l = pair("f1", [P, KD, FF])
    m.f2h, m.f2l = pair("f2", [P, FC, D])
    m.brow, m.bdup = sb("brow", [P, len(BROWS), D], F16), sb("bdup", [P, 2, 2 * D], F16)
    m.msign, m.mlow, m.mfirst, m.kconst = sb("msign", [P, 1]), sb("mlow", [P, 1]), sb("mfirst", [P, 1]), sb("kconst", [P, 1])
    m.identb, m.future = sb("identb", [P, P], BF16), sb("future", [P, P], BF16)
    m.vp = sb("vp", [P, TPB, H, Q32])
    m.nmp = sb("nmp", [P, TPB, P], F16)


def layer1(nc, a, m, out):
    with ExitStack() as c:
        def sb(name, shape, dt=F32):
            return c.enter_context(nc.sbuf_tensor(name, shape, dt))

        m.hTh, m.hTl = sb("hTh", [P, KD, N], F16), sb("hTl", [P, KD, N], F16)
        m.ctx, m.x1 = sb("ctx", [P, NT, D]), sb("x1", [P, NT, D])
        attention(nc, m)
        output_projection(nc, m)
        norm_transpose(nc, m, m.x1, m.g2, m.be2, "n2")
        feed_forward(nc, m, out)


def program(nc, a, out):
    m = Shared()
    m.xs = nc.dram_tensor("routed_rows", [(MAXBLK + N // BLK + 2) * BLK, 2 * D], F16, kind="Internal").ap()
    m.ys = nc.dram_tensor("expert_rows", [(MAXBLK + N // BLK) * BLK, D], F32, kind="Internal").ap()
    with ExitStack() as c:
        m.x = c.enter_context(nc.sbuf_tensor("x_res", [P, NT, D], F32))
        m.ident = c.enter_context(nc.sbuf_tensor("ident", [P, P], F32))
        m.ident16 = c.enter_context(nc.sbuf_tensor("ident16", [P, P], F16))
        m.mhalf = c.enter_context(nc.sbuf_tensor("mhalf", [P, KD * B], F32))
        m.ones16 = c.enter_context(nc.sbuf_tensor("ones16", [P, T], F16))
        m.slot1 = c.enter_context(nc.sbuf_tensor("slot1", [P, NT], U32))
        m.slot2 = c.enter_context(nc.sbuf_tensor("slot2", [P, NT], U32))
        m.gate1 = c.enter_context(nc.sbuf_tensor("gate1", [P, NT], F32))
        m.gate2 = c.enter_context(nc.sbuf_tensor("gate2", [P, NT], F32))
        layer1_tensors(nc, m, c)
        layer0(nc, a, m)
        layer1(nc, a, m, out)


_INS = ['x', 'itok_B_6_14', 'condB_gatescore'] + ['L0_cond_' + n for n in (
    'ln_g', 'ln_b', 'subj_emb', 'hyp_w1', 'hyp_b1', 'hyp_w2', 'hyp_b2', 'sty_w1', 'sty_b1', 'sty_w2', 'sty_b2',
    'router_w', 'exp_w1', 'exp_b1', 'exp_w2', 'exp_b2')] + ['L1_cond_' + n for n in (
        'Wq', 'bq', 'Wk', 'bk', 'Wv', 'bv', 'Wo', 'bo', 'W1', 'b1', 'W2', 'b2', 'gamma1', 'beta1', 'gamma2', 'beta2')]


def kernel(**inputs):
    import numpy as _np
    import concourse.bacc as _bacc
    from concourse import mybir as _mybir
    from concourse.bass_utils import run_bass_kernel_spmd as _run

    nc = _bacc.Bacc("TRN2", target_bir_lowering=False, num_devices=1)
    arrays, aps = {}, {}
    for name in _INS:
        arr = _np.ascontiguousarray(inputs[name])
        arrays[f"in_{name}_dram"] = arr
        aps[name] = nc.dram_tensor(f"in_{name}_dram", arr.shape, _mybir.dt.from_np(arr.dtype), kind="ExternalInput").ap()
    out = nc.dram_tensor("out_0_dram", (B, T, D), _mybir.dt.float32, kind="ExternalOutput").ap()
    program(nc, aps, out)
    r = _run(nc, [arrays], core_ids=[0])
    return r.results[0]["out_0_dram"]
```
